# Optimizing a Trainium2 kernel written in Bass

```python
import numpy as np
import jax
import jax.numpy as jnp

def _softmax(x, axis=-1):
    return jax.nn.softmax(x, axis=axis)

def _gelu(x):
    return jax.nn.gelu(x, approximate=True)

def _silu(x):
    return jax.nn.silu(x)

def _sigmoid(x):
    return jax.nn.sigmoid(x)

def _layernorm(x, axis=-1, eps=1e-05):
    m = jnp.mean(x, axis=axis, keepdims=True)
    v = jnp.var(x, axis=axis, keepdims=True)
    return (x - m) / jnp.sqrt(v + eps)

def _scatter_add(tgt, idx, src, axis=0):
    return tgt.at[idx].add(src)

def _segment_sum(src, seg, n):
    return jax.ops.segment_sum(src, seg, n)
kernel_name = 'mk_gnn_preln_d1_gnn_r8_7d2c9c'

def setup_inputs(seed: int=0):
    np.random.seed(seed)
    _w = jnp.asarray

    def _rec_inputs():
        import jax
        import jax.numpy as jnp
        _gk = jax.random.key(seed)
        x = -0.000202 + 1 * jax.random.normal(jax.random.fold_in(_gk, 1), (6250, 128), jnp.float32)
        src = jax.random.randint(jax.random.fold_in(_gk, 2), (100000,), 0, 6250, jnp.int32)
        dst = jnp.minimum((6250 * jax.random.uniform(jax.random.fold_in(_gk, 3), (100000,)) ** 2.0).astype(jnp.int32), 49999)
        _o = jnp.argsort(dst, stable=True)
        src = src[_o]
        dst = dst[_o]
        edge_type_8 = jax.random.randint(jax.random.fold_in(_gk, 12), (100000,), 0, 8, jnp.int32)
        node_type_8 = jax.random.randint(jax.random.fold_in(_gk, 13), (6250,), 0, 8, jnp.int32)
        return (x, src, dst, edge_type_8, node_type_8)
    x, src, dst, edge_type_8, node_type_8 = _rec_inputs()

    def _L0_gnn_setup():
        import jax, jax.numpy as jnp
        import numpy as np
        N = 6250
        E = 50000
        HID = 128
        H = 8
        HS = HID // H
        TN = 8
        R = 8
        L = 2
        OUT = 128
        EPS = 1e-05
        SQRT_D = float(np.sqrt(HS))

        def typed_linear(x, types, W):
            out = jnp.zeros((x.shape[0], W.shape[-1]), x.dtype)
            for t in range(W.shape[0]):
                out = out + jnp.where((types == t)[:, None], x @ W[t], 0.0)
            return out

        def rel_apply(h, etype, W):
            out = jnp.zeros_like(h)
            for r in range(W.shape[1]):
                out = out + jnp.where((etype == r)[:, None, None], jnp.einsum('ehi,hio->eho', h, W[:, r]), 0.0)
            return out

        def gt_layer(x, src, dst, ntype, etype, Wk, Wq, Wv, Wa, pri, Watt, Wmsg, skip, g, b):
            n = x.shape[0]
            k = typed_linear(x, ntype, Wk).reshape(n, H, HS)
            q = typed_linear(x, ntype, Wq).reshape(n, H, HS)
            v = typed_linear(x, ntype, Wv).reshape(n, H, HS)
            k_j, q_i, v_j = (k[src], q[dst], v[src])
            kw = rel_apply(k_j, etype, Watt)
            a = (kw * q_i).sum(-1) * pri[:, etype].T / SQRT_D
            amax = jax.ops.segment_max(a, dst, num_segments=n)
            ex = jnp.exp(a - amax[dst])
            den = jax.ops.segment_sum(ex, dst, num_segments=n)
            alpha = ex / (den[dst] + 1e-16)
            m = rel_apply(v_j, etype, Wmsg)
            agg = jax.ops.segment_sum(alpha[..., None] * m, dst, num_segments=n)
            out = jax.nn.silu(typed_linear(agg.reshape(n, HID), ntype, Wa))
            al = jax.nn.sigmoid(skip[ntype])[:, None]
            out = out * al + x * (1.0 - al)
            mu = out.mean(-1, keepdims=True)
            var = ((out - mu) ** 2).mean(-1, keepdims=True)
            return (out - mu) / jnp.sqrt(var + EPS) * g + b
        key = jax.random.key(seed)
        ks = jax.random.split(key, 12)
        s = 1.0 / np.sqrt(HID)
        sh = 1.0 / np.sqrt(HS)
        return {'x': jax.random.normal(ks[0], (N, HID), jnp.float32), 'edge_index': jax.random.randint(ks[1], (2, E), 0, N, dtype=jnp.int32), 'ntype': jax.random.randint(ks[2], (N,), 0, TN, dtype=jnp.int32), 'etype': jax.random.randint(ks[3], (E,), 0, R, dtype=jnp.int32), 'Wk': jax.random.normal(ks[4], (L, TN, HID, HID), jnp.float32) * s, 'Wq': jax.random.normal(ks[5], (L, TN, HID, HID), jnp.float32) * s, 'Wv': jax.random.normal(ks[6], (L, TN, HID, HID), jnp.float32) * s, 'Wa': jax.random.normal(ks[7], (L, TN, HID, HID), jnp.float32) * s, 'pri': jnp.ones((L, H, R), jnp.float32), 'Watt': jax.random.normal(ks[8], (L, H, R, HS, HS), jnp.float32) * sh, 'Wmsg': jax.random.normal(ks[9], (L, H, R, HS, HS), jnp.float32) * sh, 'skip': jnp.ones((L, TN), jnp.float32), 'ln_g': jnp.ones((L, HID), jnp.float32), 'ln_b': jnp.zeros((L, HID), jnp.float32), 'Wff': jax.random.normal(ks[10], (HID, OUT), jnp.float32) * s, 'bff': jnp.zeros((OUT,), jnp.float32)}
    _L0_gnn_all = _L0_gnn_setup()
    _L0_gnn_in = {k: v for k, v in _L0_gnn_all.items() if k in ('Wk', 'Wq', 'Wv', 'Wa', 'pri', 'Watt', 'Wmsg', 'skip', 'ln_g', 'ln_b', 'Wff', 'bff')}
    del _L0_gnn_all
    return {'x': x, 'src': src, 'dst': dst, 'edge_type_8': edge_type_8, 'node_type_8': node_type_8, 'L0_gnn_Wk': _L0_gnn_in['Wk'], 'L0_gnn_Wq': _L0_gnn_in['Wq'], 'L0_gnn_Wv': _L0_gnn_in['Wv'], 'L0_gnn_Wa': _L0_gnn_in['Wa'], 'L0_gnn_pri': _L0_gnn_in['pri'], 'L0_gnn_Watt': _L0_gnn_in['Watt'], 'L0_gnn_Wmsg': _L0_gnn_in['Wmsg'], 'L0_gnn_skip': _L0_gnn_in['skip'], 'L0_gnn_ln_g': _L0_gnn_in['ln_g'], 'L0_gnn_ln_b': _L0_gnn_in['ln_b'], 'L0_gnn_Wff': _L0_gnn_in['Wff'], 'L0_gnn_bff': _L0_gnn_in['bff']}

def reference(x, src, dst, edge_type_8, node_type_8, L0_gnn_Wk, L0_gnn_Wq, L0_gnn_Wv, L0_gnn_Wa, L0_gnn_pri, L0_gnn_Watt, L0_gnn_Wmsg, L0_gnn_skip, L0_gnn_ln_g, L0_gnn_ln_b, L0_gnn_Wff, L0_gnn_bff):
    import jax
    import jax.numpy as jnp

    def _L0_gnn_ref(x, edge_index, ntype, etype, Wk, Wq, Wv, Wa, pri, Watt, Wmsg, skip, ln_g, ln_b, Wff, bff):
        import jax, jax.numpy as jnp
        import numpy as np
        N = 6250
        E = 50000
        HID = 128
        H = 8
        HS = HID // H
        TN = 8
        R = 8
        L = 2
        OUT = 128
        EPS = 1e-05
        SQRT_D = float(np.sqrt(HS))

        def typed_linear(x, types, W):
            out = jnp.zeros((x.shape[0], W.shape[-1]), x.dtype)
            for t in range(W.shape[0]):
                out = out + jnp.where((types == t)[:, None], x @ W[t], 0.0)
            return out

        def rel_apply(h, etype, W):
            out = jnp.zeros_like(h)
            for r in range(W.shape[1]):
                out = out + jnp.where((etype == r)[:, None, None], jnp.einsum('ehi,hio->eho', h, W[:, r]), 0.0)
            return out

        def gt_layer(x, src, dst, ntype, etype, Wk, Wq, Wv, Wa, pri, Watt, Wmsg, skip, g, b):
            n = x.shape[0]
            k = typed_linear(x, ntype, Wk).reshape(n, H, HS)
            q = typed_linear(x, ntype, Wq).reshape(n, H, HS)
            v = typed_linear(x, ntype, Wv).reshape(n, H, HS)
            k_j, q_i, v_j = (k[src], q[dst], v[src])
            kw = rel_apply(k_j, etype, Watt)
            a = (kw * q_i).sum(-1) * pri[:, etype].T / SQRT_D
            amax = jax.ops.segment_max(a, dst, num_segments=n)
            ex = jnp.exp(a - amax[dst])
            den = jax.ops.segment_sum(ex, dst, num_segments=n)
            alpha = ex / (den[dst] + 1e-16)
            m = rel_apply(v_j, etype, Wmsg)
            agg = jax.ops.segment_sum(alpha[..., None] * m, dst, num_segments=n)
            out = jax.nn.silu(typed_linear(agg.reshape(n, HID), ntype, Wa))
            al = jax.nn.sigmoid(skip[ntype])[:, None]
            out = out * al + x * (1.0 - al)
            mu = out.mean(-1, keepdims=True)
            var = ((out - mu) ** 2).mean(-1, keepdims=True)
            return (out - mu) / jnp.sqrt(var + EPS) * g + b
        src, dst = (edge_index[0], edge_index[1])
        emb = x
        for l in range(L):
            emb = gt_layer(emb, src, dst, ntype, etype, Wk[l], Wq[l], Wv[l], Wa[l], pri[l], Watt[l], Wmsg[l], skip[l], ln_g[l], ln_b[l])
        return emb @ Wff + bff
    edge_index = jnp.stack([src, dst])
    h = jnp.maximum(_layernorm(x, axis=-1), 0.0)
    x = x + _L0_gnn_ref(h, edge_index, node_type_8, edge_type_8, L0_gnn_Wk, L0_gnn_Wq, L0_gnn_Wv, L0_gnn_Wa, L0_gnn_pri, L0_gnn_Watt, L0_gnn_Wmsg, L0_gnn_skip, L0_gnn_ln_g, L0_gnn_ln_b, L0_gnn_Wff, L0_gnn_bff)
    return x

_drawn_inputs = setup_inputs


def setup_inputs(seed=0):
    import zlib

    import numpy as np

    out = dict(_drawn_inputs(seed))
    spreads = {'L0_gnn_pri': (1.0, 0.2),
     'L0_gnn_skip': (1.0, 0.2),
     'L0_gnn_ln_g': (1.0, 0.2),
     'L0_gnn_ln_b': (0.0, 0.1),
     'L0_gnn_bff': (0.0, 0.1)}
    factors = {}
    for name, (base, spread) in spreads.items():
        noise = np.random.default_rng([zlib.crc32(name.encode()), seed]).standard_normal(out[name].shape)
        drawn = base * np.exp(spread * noise) if base else spread * noise
        out[name] = jnp.asarray(drawn.astype(out[name].dtype))
    for name, factor in factors.items():
        out[name] = (out[name] * factor).astype(out[name].dtype)
    return out
```

```python
import concourse.bass as bass
from concourse import mybir
from contextlib import ExitStack

F32 = mybir.dt.float32
BF16 = mybir.dt.bfloat16
I32 = mybir.dt.int32
ALU = mybir.AluOpType
ACT = mybir.ActivationFunctionType
AX = mybir.AxisListType

P = 128
N = 6250
E = 100000
D = 128
H = 8
HS = D // H
TN = 8
R = 8
L = 2
NT = 50
NP = NT * P
G = 14
GH = G * H
B = 56
U = 4
T = B * G
EP = T * P
Q = 112
K7 = T // Q
W = K7 * P
NB = 16
BIG = 1e30
EPS = 1e-5
XW = D + 2


class Signals(dict):

    def __init__(self, sem, stage):
        self.sem, self.stage = sem, stage

    def __missing__(self, name):
        self[name] = self.sem(f"{self.stage}_{name}")
        return self[name]


def constants(nc, sb, sem):
    c = {}
    c["ident"] = sb("ident", [P, P])
    c["row"] = sb("row_iota", [P, P])
    c["before"] = sb("before", [P, P])
    c["ones"] = sb("ones", [P, P])
    c["tile_mask"] = sb("tile_mask", [GH, G])
    c["head_of_row"] = sb("head_of_row", [GH, H])
    c["head_of_feature"] = sb("head_of_feature", [H, D])
    c["type_iota"] = sb("type_iota", [P, TN])
    c["type_iota_i"] = sb("type_iota_i", [P, P], I32)
    made, copied = sem("constants_made"), sem("constants_copied")
    with nc.Block() as block:
        @block.gpsimd
        def _(pool):
            g = nc.gpsimd
            g.memset(c["ones"][:, :], 1.0).then_inc(made, 1)
            g.iota(c["type_iota_i"][:, :], [[1, P]], base=0, channel_multiplier=0).then_inc(made, 1)
            pool.wait_ge(made, 2)
            one = c["ones"]
            g.affine_select(out=c["ident"][:, :], in_=one[:, :], compare_op=ALU.is_equal, fill=0.0, base=0,
                            pattern=[[1, P]], channel_multiplier=-1).then_inc(made, 1)
            g.affine_select(out=c["before"][:, :], in_=one[:, :], compare_op=ALU.is_ge, fill=0.0, base=-1,
                            pattern=[[1, P]], channel_multiplier=-1).then_inc(made, 1)
            g.affine_select(out=c["head_of_feature"][:, :], in_=one[0:H, :], compare_op=ALU.is_ge, fill=0.0,
                            base=0, pattern=[[1, D]], channel_multiplier=-HS).then_inc(made, 1)
            g.affine_select(out=c["tile_mask"][:, :], in_=one[0:GH, 0:G], compare_op=ALU.is_ge, fill=0.0,
                            base=0, pattern=[[-H, G]], channel_multiplier=1).then_inc(made, 1)
            pool.wait_ge(made, 6)
            g.affine_select(out=c["head_of_feature"][:, :], in_=c["head_of_feature"][:, :], compare_op=ALU.is_ge,
                            fill=0.0, base=HS - 1, pattern=[[-1, D]], channel_multiplier=HS).then_inc(made, 1)
            g.affine_select(out=c["tile_mask"][:, :], in_=c["tile_mask"][:, :], compare_op=ALU.is_ge,
                            fill=0.0, base=H - 1, pattern=[[H, G]], channel_multiplier=-1).then_inc(made, 1)

        @block.vector
        def _(dve):
            dve.wait_ge(made, 8)
            nc.vector.tensor_copy(c["row"][:, :], c["type_iota_i"][:, :]).then_inc(copied, 1)
            nc.vector.tensor_copy(c["type_iota"][:, :], c["type_iota_i"][:, 0:TN]).then_inc(copied, 1)
            nc.vector.tensor_reduce(c["head_of_row"][:, :],
                                    c["ident"][0:GH, 0:GH].rearrange("p (g h) -> p h g", h=H),
                                    axis=AX.X, op=ALU.add).then_inc(copied, 1)
    return c


def edge_lists(nc, sem, dst, src, etype, edge_dst, edge_key, unsorted):
    full = E // W
    rest = E - full * W
    loaded, filled, keyed, stored, counted, summed = (sem(f"lists_{x}") for x in (
        "loaded", "filled", "keyed", "stored", "counted", "summed"))
    with ExitStack() as st:
        sb = lambda n, s, d=F32: st.enter_context(nc.sbuf_tensor(n, s, d))
        dsts, srcs, rels, prev = (sb(f"l_{x}", [Q, W], I32) for x in ("dst", "src", "rel", "prev"))
        lead = sb("l_lead", [1, 1], I32)
        falls, count, one = sb("l_falls", [Q, W]), sb("l_count", [Q, 1]), sb("l_one", [Q, 1])
        ps = st.enter_context(nc.psum_tensor("l_ps", [1, 1], F32))
        with nc.Block() as block:
            @block.sync
            def _(sp):
                sp.wait_ge(filled, 4)
                for to, of in ((dsts, dst), (srcs, src), (rels, etype)):
                    sp.dma_start(to[0:full, :], of[0:full * W].rearrange("(p w) -> p w", w=W)).then_inc(loaded, 16)
                    sp.dma_start(to[full:full + 1, 0:rest], of[full * W:E].rearrange("(p w) -> p w", p=1)).then_inc(loaded, 16)
                sp.wait_ge(loaded, 96)
                sp.dma_start(edge_dst[1:EP + 1].rearrange("(p w) -> p w", w=W), dsts[:, :]).then_inc(stored, 16)
                sp.dma_start(edge_dst[0:1].rearrange("(p w) -> p w", p=1), lead[:, :]).then_inc(stored, 16)
                sp.wait_ge(keyed, 1)
                sp.dma_start(edge_key.rearrange("(p w) -> p w", w=W), srcs[:, :]).then_inc(stored, 16)
                sp.wait_ge(stored, 48)
                sp.dma_start(prev[:, :], edge_dst[0:EP].rearrange("(p w) -> p w", w=W)).then_inc(loaded, 16)

            @block.vector
            def _(dve):
                v = nc.vector
                v.memset(dsts[:, :], N).then_inc(filled, 1)
                v.memset(srcs[:, :], 0).then_inc(filled, 1)
                v.memset(rels[:, :], 0).then_inc(filled, 1)
                v.memset(lead[:, :], -1).then_inc(filled, 1)
                v.memset(one[:, :], 1.0).then_inc(filled, 1)
                dve.wait_ge(loaded, 96)
                v.scalar_tensor_tensor(out=srcs[:, :], in0=srcs[:, :], scalar=float(R), in1=rels[:, :],
                                       op0=ALU.mult, op1=ALU.add).then_inc(keyed, 1)
                dve.wait_ge(loaded, 112)
                v.tensor_tensor(falls[:, :], prev[:, :], dsts[:, :], ALU.is_gt).then_inc(counted, 1)
                dve.wait_ge(counted, 1)
                v.reduce_sum(count[:, :], falls[:, :], axis=AX.X).then_inc(counted, 1)
                dve.wait_ge(summed, 1)
                v.tensor_copy(unsorted[:, :], ps[:, :]).then_inc(counted, 1)

            @block.tensor
            def _(pe):
                pe.wait_ge(filled, 5)
                pe.wait_ge(counted, 2)
                nc.tensor.matmul(ps[:, :], count[:, :], one[:, :], start=True, stop=True).then_inc(summed, 1)


def edge_sort(nc, c, sem, edge_dst, edge_key, unsorted, slots):
    s = Signals(sem, "sort")
    C1, C2 = 10, 6
    with ExitStack() as st:
        sb = lambda n, sh, d=F32: st.enter_context(nc.sbuf_tensor(f"s_{n}", sh, d))
        dst, key = sb("dst", [P, T], I32), sb("key", [P, T], I32)
        dstf, number = sb("dstf", [P, T]), sb("number", [P, T])
        after, diag, same = sb("after", [P, P]), sb("diag", [P, P]), sb("same", [P, P])
        zero, count, run = sb("zero", [P, NT]), sb("count", [P, NT]), sb("run", [P, NT])
        col, rank, total, held, place = (sb(n, [P, 1]) for n in ("col", "rank", "total", "held", "place"))
        idx, key_c, to, to1 = (sb(n, [P, 1], I32) for n in ("idx", "key_c", "to", "to1"))
        ps = st.enter_context(nc.psum_tensor("s_ps", [P, P], F32))
        ps1 = st.enter_context(nc.psum_tensor("s_ps1", [P, 1], F32))
        by_edge = lambda a: a.rearrange("(p t) -> p t", t=T)
        by_node = slots.rearrange("(p t) o -> p (t o)", t=NT)

        def where_unsorted(engine):
            flag = engine.alloc_register("unsorted")
            engine.reg_load(flag, unsorted[0:1, 0:1])
            return engine.If(engine.snap(flag, min_val=0, max_val=EP) > 0)

        with nc.Block() as block:
            @block.sync
            def _(sp):
                with where_unsorted(sp):
                    sp.dma_start(dst[:, :], by_edge(edge_dst[1:EP + 1])).then_inc(s["loaded"], 16)
                    sp.dma_start(key[:, :], by_edge(edge_key)).then_inc(s["loaded"], 16)
                    sp.wait_ge(s["dv"], 1)
                    sp.dma_start(by_node, zero[:, :]).then_inc(s["slots"], 16)
                    sp.wait_ge(s["put"], 16 * T)
                    sp.dma_start(count[:, :], by_node).then_inc(s["loaded"], 16)
                    sp.wait_ge(s["dv"], 4 + T * C1 + 3)
                    sp.dma_start(by_node, run[:, :]).then_inc(s["slots"], 16)
                    sp.wait_ge(s["slots"], 32)

            @block.vector
            def _(dve):
                v = nc.vector

                def chain(at):
                    k = [0]

                    def then(ins, wait=True):
                        k[0] += 1
                        ins.then_inc(s["dv"], 1)
                        if wait:
                            dve.wait_ge(s["dv"], at + k[0])
                    return then

                with where_unsorted(dve):
                    then = chain(0)
                    then(v.memset(zero[:, :], 0.0))
                    then(v.tensor_tensor(after[:, :], c["ones"][:, :], c["before"][:, :], ALU.subtract))
                    then(v.tensor_tensor(after[:, :], after[:, :], c["ident"][:, :], ALU.subtract))
                    dve.wait_ge(s["loaded"], 32)
                    then(v.tensor_copy(dstf[:, :], dst[:, :]))
                    with dve.Fori(0, T) as t:
                        dve.wait_ge(s["go"], t * 3 + 1)
                        then = chain(t * C1 + 4)
                        then(v.tensor_copy(col[:, :], dstf[:, bass.ds(t, 1)]))
                        then(v.tensor_copy(idx[:, :], dst[:, bass.ds(t, 1)]))
                        then(v.tensor_scalar(diag[:, :], c["ident"][:, :], col[:, 0:1], None, ALU.mult))
                        dve.wait_ge(s["pe"], t + 1)
                        then(v.tensor_scalar(same[:, :], ps[:, :], col[:, 0:1], None, ALU.is_equal))
                        then(v.reduce_sum(total[:, :], same[:, :], axis=AX.X))
                        then(v.tensor_tensor(same[:, :], same[:, :], after[:, :], ALU.mult))
                        then(v.reduce_sum(rank[:, :], same[:, :], axis=AX.X))
                        dve.wait_ge(s["got"], (t + 1) * 16)
                        then(v.tensor_tensor(rank[:, :], rank[:, :], held[:, :], ALU.add))
                        then(v.tensor_copy(number[:, bass.ds(t, 1)], rank[:, :]))
                        then(v.tensor_tensor(total[:, :], total[:, :], held[:, :], ALU.add), wait=False)
                    then = chain(4 + T * C1)
                    dve.wait_ge(s["loaded"], 48)
                    then(v.tensor_tensor_scan(run[:, :], count[:, :], count[:, :], 0.0, ALU.add, ALU.max))
                    dve.wait_ge(s["pe"], T + 1)
                    then(v.tensor_scalar(run[:, :], run[:, :], ps1[:, 0:1], None, ALU.add))
                    then(v.tensor_tensor(run[:, :], run[:, :], count[:, :], ALU.subtract))
                    with dve.Fori(0, T) as t:
                        dve.wait_ge(s["go"], (t + T) * 3 + 2)
                        then = chain(t * C2 + (4 + T * C1 + 3))
                        then(v.tensor_copy(idx[:, :], dst[:, bass.ds(t, 1)]))
                        then(v.tensor_copy(key_c[:, :], key[:, bass.ds(t, 1)]))
                        then(v.tensor_copy(rank[:, :], number[:, bass.ds(t, 1)]))
                        dve.wait_ge(s["got"], (t + T + 1) * 16)
                        then(v.tensor_tensor(place[:, :], held[:, :], rank[:, :], ALU.add))
                        then(v.tensor_copy(to[:, :], place[:, :]))
                        then(v.tensor_scalar(to1[:, :], place[:, :], 1.0, None, ALU.add), wait=False)
                    v.memset(zero[:, :], 0.0).then_inc(s["dv"], 1)

            @block.tensor
            def _(pe):
                with where_unsorted(pe):
                    with pe.Fori(0, T) as t:
                        pe.wait_ge(s["dv"], t * C1 + 7)
                        nc.tensor.matmul(ps[:, :], c["ones"][:, :], diag[:, :], start=True, stop=True).then_inc(s["pe"], 1)
                    pe.wait_ge(s["dv"], 4 + T * C1 + 1)
                    nc.tensor.matmul(ps1[:, :], c["before"][:, :], run[:, NT - 1:NT], start=True, stop=True).then_inc(s["pe"], 1)

            @block.gpsimd
            def _(pool):
                g = nc.gpsimd
                at = lambda ap: bass.IndirectOffsetOnAxis(ap=ap[:, 0:1], axis=0)

                def ready():
                    pool.sem_inc(s["go"], 1)

                with where_unsorted(pool):
                    pool.wait_ge(s["slots"], 16)
                    ready()
                    with pool.Fori(0, T) as t:
                        pool.wait_ge(s["dv"], t * C1 + 6)
                        ready()
                        g.indirect_dma_start(out=held[:, :], out_offset=None, in_=slots[:, :], in_offset=at(idx)).then_inc(s["got"], 16)
                        pool.wait_ge(s["dv"], t * C1 + (4 + C1))
                        ready()
                        g.indirect_dma_start(out=slots[:, :], out_offset=at(idx), in_=total[:, :], in_offset=None).then_inc(s["put"], 16)
                        pool.wait_ge(s["put"], (t + 1) * 16)
                        ready()
                    pool.wait_ge(s["slots"], 32)
                    ready()
                    with pool.Fori(0, T) as t:
                        pool.wait_ge(s["dv"], t * C2 + (4 + T * C1 + 4))
                        ready()
                        g.indirect_dma_start(out=held[:, :], out_offset=None, in_=slots[:, :], in_offset=at(idx)).then_inc(s["got"], 16)
                        pool.wait_ge(s["dv"], t * C2 + (4 + T * C1 + 3 + C2))
                        ready()
                        g.indirect_dma_start(out=edge_dst.rearrange("(e o) -> e o", o=1), out_offset=at(to1), in_=idx[:, :],
                                             in_offset=None).then_inc(s["put"], 16)
                        g.indirect_dma_start(out=edge_key.rearrange("(e o) -> e o", o=1), out_offset=at(to), in_=key_c[:, :],
                                             in_offset=None).then_inc(s["put"], 16)
                        pool.wait_ge(s["put"], (t * 2 + T + 2) * 16)
                        ready()
                    pool.wait_ge(s["put"], 16 * 3 * T)
                    ready()


def edge_tables(nc, c, sem, x, ntype, edge_dst, edge_key, tab, scratch):
    s = Signals(sem, "tables")
    with ExitStack() as st:
        sb = lambda n, sh, d=F32: st.enter_context(nc.sbuf_tensor(n, sh, d))
        cur, prev, key, lo_i, hi_i = (sb(f"e_{n}", [Q, W], I32) for n in ("cur", "prev", "key", "lo_i", "hi_i"))
        start, cid, rank, keyf, lo, hi = (sb(f"e_{n}", [Q, W]) for n in ("start", "cid", "rank", "keyf", "lo", "hi"))
        base, w0 = sb("e_base", [Q, 1]), sb("e_w0", [Q, K7])
        w0_i = sb("e_w0_i", [Q, K7], I32)
        new_f, pas_f = sb("e_new", [Q, K7], BF16), sb("e_pas", [Q, K7], BF16)
        lo_t, hi_t = sb("e_lo_t", [P, T], BF16), sb("e_hi_t", [P, T], BF16)
        row_b = sb("e_row_b", [P, P], BF16)
        hot_lo = [sb(f"e_hot_lo{u}", [P, G, P], BF16) for u in range(2)]
        hot_hi = [sb(f"e_hot_hi{u}", [P, G, NT], BF16) for u in range(2)]
        zero_b = sb("e_zero_b", [P, P], BF16)
        has, pre, tot, run, num, cf = (sb(f"e_{n}", [P, NT]) for n in ("has", "pre", "tot", "run", "num", "cf"))
        nt_i, n_i, compact = sb("e_nt_i", [P, NT], I32), sb("e_n_i", [P, NT], I32), sb("e_compact", [P, NT], I32)
        lrb = sb("e_lrb", [GH, B, P])
        xr = sb("e_xr", [P, NT, XW])
        ps_t = [st.enter_context(nc.psum_tensor(f"e_ps_t{u}", [P, K7 + 1, P], F32)) for u in range(2)]
        ps_h = st.enter_context(nc.psum_tensor("e_ps_h", [P, NT], F32))
        ps_s = st.enter_context(nc.psum_tensor("e_ps_s", [P, 256], F32))
        full = N // P
        rest = N - full * P
        HALF = B // 2
        tiles_of = lambda a: a[:, :].rearrange("p (q k) -> p k q", k=K7)
        with nc.Block() as block:
            @block.sync
            def _(sp):
                sp.dma_start(cur[:, :], edge_dst[1:EP + 1].rearrange("(p w) -> p w", w=W)).then_inc(s["loaded"], 16)
                sp.dma_start(prev[:, :], edge_dst[0:EP].rearrange("(p w) -> p w", w=W)).then_inc(s["loaded"], 16)
                sp.dma_start(key[:, :], edge_key.rearrange("(p w) -> p w", w=W)).then_inc(s["loaded"], 16)
                sp.wait_ge(s["filled"], 2)
                sp.dma_start(xr[:, 0:full, 0:D], x[0:full * P, :].rearrange("(t p) d -> p t d", p=P)).then_inc(s["nodes_in"], 16)
                sp.dma_start(xr[0:rest, full, 0:D], x[full * P:N, :]).then_inc(s["nodes_in"], 16)
                with nc.allow_non_contiguous_dma(reason="one word for each node, once"):
                    sp.dma_start(nt_i[:, 0:full], ntype[0:full * P].rearrange("(t p) -> p t", p=P)).then_inc(s["nodes_in"], 16)
                    sp.dma_start(nt_i[0:rest, full:full + 1], ntype[full * P:N].rearrange("(p o) -> p o", o=1)).then_inc(s["nodes_in"], 16)
                sp.wait_ge(s["dv"], 12)
                w0_d = scratch["w0"].rearrange("(b s) -> b s", s=NB)
                with nc.allow_non_contiguous_dma(reason="a few words, once"):
                    sp.dma_start(w0_d[:, 0:K7], w0_i[0:Q:2, :]).then_inc(s["stored"], 16)
                    sp.dma_start(w0_d[:, K7:G], w0_i[1:Q:2, :]).then_inc(s["stored"], 16)
                    sp.dma_start(w0_d[:, G:NB], w0_i[0:Q:2, 0:NB - G]).then_inc(s["stored"], 16)
                sp.dma_start(scratch["rank"].rearrange("(p w) -> p w", w=W), rank[:, :]).then_inc(s["stored"], 16)
                sp.dma_start(scratch["new"].rearrange("(p w) -> p w", w=K7), new_f[:, :]).then_inc(s["stored"], 16)
                sp.dma_start(scratch["pas"].rearrange("(p w) -> p w", w=K7), pas_f[:, :]).then_inc(s["stored"], 16)
                sp.wait_ge(s["stored"], 96)
                sp.dma_start(tab["w0"][:, :], scratch["w0"].rearrange("(p w) -> p w", p=1)).then_inc(s["rows_in"], 16)
                for to, of in ((tab["new"], scratch["new"]), (tab["pass"], scratch["pas"])):
                    sp.dma_start(to[:, :], of.rearrange("(p w) -> p w", p=1).to_broadcast([H, T])).then_inc(s["rows_in"], 16)
                rank_d = scratch["rank"].rearrange("(b g o e) -> g o b e", g=G, e=P, o=1)
                for g in range(G):
                    sp.dma_start(lrb[g * H:(g + 1) * H, :, :], rank_d[g].to_broadcast([H, B, P])).then_inc(s["lrb_in"], 16)
                sp.wait_ge(s["rows_in"], 48)

            @block.vector
            def _(dve):
                v = nc.vector
                n = [0]

                def did(ins):
                    ins.then_inc(s["dv"], 1)
                    n[0] += 1

                def then(ins):
                    did(ins)
                    dve.wait_ge(s["dv"], n[0])

                dve.wait_ge(s["loaded"], 48)
                did(v.tensor_tensor(start[:, :], cur[:, :], prev[:, :], ALU.not_equal))
                did(v.tensor_copy(keyf[:, :], key[:, :]))
                did(v.tensor_scalar(lo_i[:, :], cur[:, :], P - 1, None, ALU.bitwise_and))
                then(v.tensor_scalar(hi_i[:, :], cur[:, :], 7, None, ALU.arith_shift_right))
                did(v.tensor_copy(lo[:, :], lo_i[:, :]))
                did(v.tensor_copy(hi[:, :], hi_i[:, :]))
                then(v.tensor_tensor_scan(cid[:, :], start[:, :], start[:, :], 0.0, ALU.add, ALU.max))
                dve.wait_ge(s["pe"], 1)
                then(v.tensor_scalar(cid[:, :], cid[:, :], ps_s[0:Q, 0:1], -1.0, ALU.add, ALU.add))
                c3 = cid[:, :].rearrange("p (k e) -> p k e", e=P)
                r3 = rank[:, :].rearrange("p (k e) -> p k e", e=P)
                s3 = start[:, :].rearrange("p (k e) -> p k e", e=P)
                did(v.tensor_copy(w0_i[:, :], c3[:, :, 0]))
                then(v.tensor_tensor(r3, c3, c3[:, :, 0:1].to_broadcast([Q, K7, P]), ALU.subtract))
                then(v.tensor_scalar(new_f[:, :], s3[:, :, 0], -BIG, None, ALU.mult))
                did(v.scalar_tensor_tensor(out=pas_f[:, :], in0=r3[:, :, P - 1], scalar=-BIG, in1=new_f[:, :],
                                           op0=ALU.mult, op1=ALU.add))
                then(v.tensor_copy(row_b[:, :], c["row"][:, :]))
                dve.wait_ge(s["pe"], 2)
                did(v.tensor_copy(tiles_of(tab["rank"]), ps_t[0][:, 0:K7, 0:Q]))
                dve.wait_ge(s["pe"], 3)
                did(v.tensor_copy(tiles_of(tab["key"]), ps_t[1][:, 0:K7, 0:Q]))
                dve.wait_ge(s["pe"], 4)
                did(v.tensor_copy(tiles_of(lo_t), ps_t[0][:, 0:K7, 0:Q]))
                dve.wait_ge(s["pe"], 5)
                then(v.tensor_copy(tiles_of(hi_t), ps_t[1][:, 0:K7, 0:Q]))

                def hots(b, u, i):
                    if i is not None:
                        dve.wait_ge(s["counted"], b - 1)
                    v.tensor_tensor(hot_lo[u][:, :, :], row_b[:, :].rearrange("p (o e) -> p o e", o=1).to_broadcast([P, G, P]),
                                    lo_t[:, bass.ds(b * G, G)].rearrange("p (g o) -> p g o", o=1).to_broadcast([P, G, P]),
                                    ALU.is_equal).then_inc(s["hot"], 1)
                    v.tensor_tensor(hot_hi[u][:, :, :], row_b[:, 0:NT].rearrange("p (o e) -> p o e", o=1).to_broadcast([P, G, NT]),
                                    hi_t[:, bass.ds(b * G, G)].rearrange("p (g o) -> p g o", o=1).to_broadcast([P, G, NT]),
                                    ALU.is_equal).then_inc(s["hot"], 1)

                hots(0, 0, None)
                hots(1, 1, None)
                with dve.Fori(1, HALF) as i:
                    hots(i * 2, 0, i)
                    hots(i * 2 + 1, 1, i)
                dve.wait_ge(s["counted"], B + 1)
                then(v.tensor_scalar(has[:, :], ps_h[:, :], 1.0, None, ALU.min))
                dve.wait_ge(s["filled"], 4)
                did(v.tensor_copy(num[:, :], n_i[:, :]))
                dve.wait_ge(s["pe"], 6)
                did(v.tensor_copy(pre[:, :], ps_s[:, 64:64 + NT]))
                then(v.tensor_copy(tot[:, :], ps_s[:, 128:128 + NT]))
                then(v.tensor_tensor_scan(run[:, :], tot[:, :], tot[:, :], 0.0, ALU.add, ALU.max))
                then(v.tensor_tensor(pre[:, :], pre[:, :], run[:, :], ALU.add))
                then(v.tensor_tensor(pre[:, :], pre[:, :], tot[:, :], ALU.subtract))
                then(v.tensor_tensor(cf[:, :], num[:, :], pre[:, :], ALU.subtract))
                then(v.tensor_scalar(cf[:, :], cf[:, :], run[:, NT - 1:NT], None, ALU.add))
                then(v.tensor_tensor(pre[:, :], pre[:, :], cf[:, :], ALU.subtract))
                then(v.tensor_tensor(pre[:, :], pre[:, :], has[:, :], ALU.mult))
                then(v.tensor_tensor(compact[:, :], cf[:, :], pre[:, :], ALU.add))
                dve.wait_ge(s["nodes_in"], 64)
                did(v.tensor_copy(xr[:, :, D], nt_i[:, :]))
                did(v.tensor_copy(xr[:, :, D + 1], num[:, :]))
                dve.wait_ge(s["lrb_in"], 16 * G)
                did(v.tensor_scalar(tab["first"][:, :, :], lrb[:, :, :], 1.0, -BIG, ALU.min, ALU.mult))
                then(v.memset(tab["seam"][:, :, :], 0.0))
                then(v.tensor_tensor(tab["seam"][:, :, 1:P], lrb[:, :, 1:P], lrb[:, :, 0:P - 1], ALU.subtract))
                did(v.tensor_scalar(tab["seam"][:, :, 1:P], tab["seam"][:, :, 1:P], -BIG, None, ALU.mult))

            @block.tensor
            def _(pe):
                t = nc.tensor
                pe.wait_ge(s["dv"], 7)
                t.matmul(ps_s[0:Q, 0:1], c["before"][0:Q, 0:Q], cid[:, W - 1:W], start=True, stop=True).then_inc(s["pe"], 1)
                for i, a in enumerate((rank, keyf, lo, hi)):
                    pe.wait_ge(s["dv"], (10, 10, 14, 15)[i])
                    for k in range(K7):
                        last = t.transpose(ps_t[i % 2][:, k, 0:Q], a[:, k * P:(k + 1) * P], c["ident"][0:Q, 0:Q])
                    last.then_inc(s["pe"], 1)
                pe.wait_ge(s["filled"], 3)
                t.matmul(ps_h[:, :], zero_b[:, :], zero_b[:, 0:NT], start=True, stop=False)

                def count(b, u):
                    pe.wait_ge(s["hot"], b * 2 + 2)
                    for g in range(G):
                        last = t.matmul(ps_h[:, :], hot_lo[u][:, g, :], hot_hi[u][:, g, :], start=False, stop=False)
                    last.then_inc(s["counted"], 1)

                with pe.Fori(0, HALF) as i:
                    count(i * 2, 0)
                    count(i * 2 + 1, 1)
                t.matmul(ps_h[:, :], zero_b[:, :], zero_b[:, 0:NT], start=False, stop=True).then_inc(s["counted"], 1)
                pe.wait_ge(s["dv"], 18)
                t.matmul(ps_s[:, 64:64 + NT], c["before"][:, :], has[:, :], start=True, stop=True)
                t.matmul(ps_s[:, 128:128 + NT], c["ones"][:, :], has[:, :], start=True, stop=True).then_inc(s["pe"], 1)

            @block.gpsimd
            def _(pool):
                g = nc.gpsimd
                g.memset(xr[:, :, :], 0.0).then_inc(s["filled"], 1)
                g.memset(nt_i[:, :], 0).then_inc(s["filled"], 1)
                g.memset(zero_b[:, :], 0.0).then_inc(s["filled"], 1)
                g.iota(n_i[:, :], [[P, NT]], base=0, channel_multiplier=1).then_inc(s["filled"], 1)
                pool.wait_ge(s["dv"], 31)
                for i in range(NT):
                    g.indirect_dma_start(out=scratch["rows"][:, :], out_offset=bass.IndirectOffsetOnAxis(ap=compact[:, i:i + 1], axis=0),
                                         in_=xr[:, i, :], in_offset=None).then_inc(s["scattered"], 16)
                pool.wait_ge(s["scattered"], 16 * NT)



def node_stage(nc, c, sem, l, tab, scratch, acc, weights, out):
    s = Signals(sem, f"nodes{l}")
    put_out = [s[f"put{u}"] for u in range(2)]
    q_out = [s[f"q_out{u}"] for u in range(2)] if l < L else None
    sqrt_at, bd_at, h_at = [], [], []
    first, last = l == 0, l == L
    with ExitStack() as st:
        sb = lambda n, sh, d=F32: st.enter_context(nc.sbuf_tensor(f"n{l}_{n}", sh, d))
        pb = lambda n, sh: st.enter_context(nc.psum_tensor(f"n{l}_{n}", sh, F32))
        h = sb("h", [P, NT, D])
        sq = acc[:, 1, :].rearrange("p (t d) -> p t d", d=D)
        st1, st2 = sb("st1", [P, NT]), sb("st2", [P, NT])
        if first or last:
            xr = sb("xr", [P, NT, XW])
        if not first:
            old = sb("old", [P, NT, D])
            skip, al, gain, shift = sb("skip", [P, TN]), sb("al", [P, NT]), sb("gain", [P, D]), sb("shift", [P, D])
            agg = [sb(f"agg{u}", [P, P]) for u in range(2)]
        ids = [sb(f"ids{u}", [P, 1], I32) for u in range(2)]
        hm = [sb(f"hm{u}", [P, TN, D]) for u in range(2)]
        ht = [sb(f"ht{u}", [P, TN, P]) for u in range(2)]
        prod = hm
        if not last:
            wk, wv, wq = (sb(n, [P, TN, D]) for n in ("wk", "wv", "wq"))
            bd = [sb(f"bd{i}", [P, R, D]) for i in range(2)]
            pri = sb("pri", [P, R])
            kv_t = [sb(f"kv_t{u}", [P, 2, P]) for u in range(2)]
            q_sb = [sb(f"q_sb{u}", [P, D]) for u in range(2)]
            kv = [sb(f"kv{u}", [P, R, 2, D]) for u in range(2)]
            wa = kv[0][:, 0:TN // 2, :, :].rearrange("p a b d -> p (a b) d")
        else:
            wa = sb("wa", [P, TN, D])[:, :, :]
            wff, bff = sb("wff", [P, D]), sb("bff", [P, D])
            y = [sb(f"y{u}", [P, D]) for u in range(2)]
        ps_a, ps_b = pb("ps_a", [P, TN, P]), pb("ps_b", [P, 2, 512])
        ps_c, ps_d = pb("ps_c", [P, R, D]), pb("ps_d", [P, 2, 512])

        with nc.Block() as block:
            @block.vector
            def _(dve):
                v = nc.vector
                n = [0]

                def did(ins):
                    ins.then_inc(s["dv"], 1)
                    n[0] += 1

                def then(ins):
                    did(ins)
                    dve.wait_ge(s["dv"], n[0])

                def each(a):
                    return a[:, :].rearrange("p (t o) -> p t o", o=1).to_broadcast([P, NT, D])

                def all_nodes(a):
                    return a[:, :].rearrange("p (o d) -> p o d", o=1).to_broadcast([P, NT, D])

                def norm(of):
                    then(v.reduce_sum(st1[:, :], of, axis=AX.X))
                    then(v.tensor_scalar(st1[:, :], st1[:, :], -1.0 / D, None, ALU.mult))
                    then(v.tensor_tensor(h[:, :, :], of, each(st1), ALU.add))
                    then(v.tensor_tensor(sq, h[:, :, :], h[:, :, :], ALU.mult))
                    then(v.reduce_sum(st1[:, :], sq, axis=AX.X))
                    did(v.tensor_scalar(st2[:, :], st1[:, :], 1.0 / D, EPS, ALU.mult, ALU.add))
                    sqrt_at.append(n[0])
                    dve.wait_ge(s["act"], 1 if first else 3)
                    then(v.reciprocal(st2[:, :], st2[:, :]))
                    then(v.tensor_tensor(h[:, :, :], h[:, :, :], each(st2), ALU.mult))

                if not last:
                    v.memset(bd[0][:, :, :], 0.0).then_inc(s["built"], 1)
                    v.memset(bd[1][:, :, :], 0.0).then_inc(s["built"], 1)
                if first:
                    dve.wait_ge(s["rows"], 16)
                    did(v.tensor_copy(tab["id"][:, :], xr[:, :, D + 1]))
                    then(v.tensor_tensor(tab["type"][:, :, :], xr[:, :, D:D + 1].to_broadcast([P, NT, TN]),
                                         c["type_iota"][:, :].rearrange("p (o t) -> p o t", o=1).to_broadcast([P, NT, TN]),
                                         ALU.is_equal))
                    norm(xr[:, :, 0:D])
                    did(v.tensor_scalar(h[:, :, :], h[:, :, :], 0.0, None, ALU.max))
                else:
                    then(v.tensor_scalar(acc[:, 1, :], acc[:, 1, :], 1e-16, None, ALU.add))
                    then(v.reciprocal(acc[:, 1, :], acc[:, 1, :]))

                    def scale(t, u):
                        v.tensor_tensor(agg[u][:, :], acc[:, 0, bass.ds(t * P, P)], acc[:, 1, bass.ds(t * P, P)],
                                        ALU.mult).then_inc(s["agg"], 1)

                    def pick(t, u):
                        dve.wait_ge(s["lin"], t + 1)
                        ps = (ps_a, ps_c)[u]
                        v.tensor_tensor(prod[u][:, :, :], ps[:, :, :],
                                        tab["type"][:, bass.ds(t, 1), :].rearrange("p o t -> p t o").to_broadcast([P, TN, D]),
                                        ALU.mult).then_inc(s["prod"], 1)
                        dve.wait_ge(s["prod"], t * 2 + 1)
                        v.tensor_reduce(h[:, bass.ds(t, 1), :].rearrange("p o d -> p (o d)"),
                                        prod[u][:, :, :].rearrange("p t d -> p d t"), axis=AX.X, op=ALU.add).then_inc(s["prod"], 1)

                    scale(0, 0)
                    scale(1, 1)
                    with dve.Fori(0, NT // 2 - 1) as i:
                        for u in range(2):
                            pick(i * 2 + u, u)
                            scale(i * 2 + u + 2, u)
                    pick(NT - 2, 0)
                    pick(NT - 1, 1)
                    dve.wait_ge(s["w"], 64)
                    then(v.tensor_tensor(sq[:, :, 0:TN], tab["type"][:, :, :],
                                         skip[:, :].rearrange("p (o t) -> p o t", o=1).to_broadcast([P, NT, TN]), ALU.mult))
                    did(v.reduce_sum(al[:, :], sq[:, :, 0:TN], axis=AX.X))
                    sqrt_at.append(n[0])
                    dve.wait_ge(s["rows"], 32 if last else 16)
                    dve.wait_ge(s["act"], 2)
                    then(v.tensor_tensor(h[:, :, :], h[:, :, :], old[:, :, :], ALU.subtract))
                    then(v.tensor_tensor(h[:, :, :], h[:, :, :], each(al), ALU.mult))
                    then(v.tensor_tensor(h[:, :, :], h[:, :, :], old[:, :, :], ALU.add))
                    norm(h[:, :, :])
                    then(v.tensor_tensor(h[:, :, :], h[:, :, :], all_nodes(gain), ALU.mult))
                    did(v.tensor_tensor(h[:, :, :], h[:, :, :], all_nodes(shift), ALU.add))
                h_at.append(n[0])
                dve.wait_ge(s["dv"], n[0])
                if last:
                    dve.wait_ge(s["w_ff"], 32)
                    then(v.tensor_tensor(xr[:, :, 0:D], xr[:, :, 0:D], all_nodes(bff), ALU.add))

                    def stage(t, u):
                        v.tensor_copy(hm[u][:, 0, :], h[:, bass.ds(t, 1), :].rearrange("p o d -> p (o d)")).then_inc(s["hm"], 1)

                    def result(i, u, peeled=False):
                        t = i * 2 + u
                        dve.wait_ge(s["qkv"], t + 1)
                        if not peeled:
                            dve.wait_ge(put_out[u], i * 16)
                        v.tensor_tensor(y[u][:, :], (ps_c, ps_d)[u][:, 0, 0:D],
                                        xr[:, bass.ds(t, 1), 0:D].rearrange("p o d -> p (o d)"), ALU.add).then_inc(s["qkv_sb"], 1)

                    stage(0, 0)
                    stage(1, 1)
                    result(0, 0, True)
                    stage(2, 0)
                    result(0, 1, True)
                    stage(3, 1)
                    with dve.Fori(1, NT // 2 - 1) as i:
                        for u in range(2):
                            result(i, u)
                            stage(i * 2 + u + 2, u)
                    result(NT // 2 - 1, 0)
                    result(NT // 2 - 1, 1)
                    return
                dve.wait_ge(s["bd"], 16 * (3 * H))
                then(v.tensor_scalar(pri[:, :], pri[:, :], float(HS) ** -0.5, None, ALU.mult))
                then(v.tensor_tensor(bd[0][:, :, :], bd[0][:, :, :],
                                     pri[:, :].rearrange("p (r o) -> p r o", o=1).to_broadcast([P, R, D]), ALU.mult))
                bd_at.append(n[0])

                def split(t, u, peeled):
                    if not peeled:
                        dve.wait_ge(s["tp"], t - 1)
                    v.tensor_tensor(hm[u][:, :, :], h[:, bass.ds(t, 1), :].to_broadcast([P, TN, D]),
                                    tab["type"][:, bass.ds(t, 1), :].rearrange("p o t -> p t o").to_broadcast([P, TN, D]),
                                    ALU.mult).then_inc(s["hm"], 1)

                def take(i, u, ahead=True, peeled=False):
                    t = i * 2 + u
                    dve.wait_ge(s["qkv"], t + 1)
                    v.tensor_copy(kv_t[u][:, :, :], ps_b[:, 0, 0:2 * P].rearrange("p (a n) -> p a n", a=2)).then_inc(s["rel_v"], 1)
                    if ahead:
                        split(t + 2, u, False)
                    if not peeled:
                        dve.wait_ge(put_out[u], i * 16)
                    dve.wait_ge(s["rel"], t * 2 + 2)
                    v.tensor_copy(kv[u][:, :, 1, :], ps_d[:, :, :].rearrange("p a (r d) -> p (a r) d", d=D)).then_inc(s["rel_v"], 1)

                split(0, 0, True)
                split(1, 1, True)
                take(0, 0, peeled=True)
                take(0, 1, peeled=True)
                with dve.Fori(1, NT // 2 - 1) as i:
                    for u in range(2):
                        take(i, u)
                take(NT // 2 - 1, 0, ahead=False)
                take(NT // 2 - 1, 1, ahead=False)

            @block.sync
            def _(sp):
                def load(to, of, sm):
                    sp.dma_start(to, of).then_inc(sm, 16)

                tiles = lambda a: a.rearrange("(t p) d -> p t d", p=P)
                if first or last:
                    load(xr[:, :, :], tiles(scratch["rows"]), s["rows"])
                if not first:
                    load(old[:, :, :], tiles(scratch["h"]), s["rows"])
                    load(wa[:, :, :], weights["Wa"][l - 1].rearrange("t i o -> i t o"), s["w"])
                    load(skip[:, :], weights["skip"][l - 1:l, :].to_broadcast([P, TN]), s["w"])
                    load(gain[:, :], weights["ln_g"][l - 1:l, :].to_broadcast([P, D]), s["w"])
                    load(shift[:, :], weights["ln_b"][l - 1:l, :].to_broadcast([P, D]), s["w"])
                if last:
                    load(wff[:, :], weights["Wff"], s["w_ff"])
                    load(bff[:, :], weights["bff"].rearrange("(o d) -> o d", o=1).to_broadcast([P, D]), s["w_ff"])
                else:
                    for to, name in ((wk, "Wk"), (wv, "Wv"), (wq, "Wq")):
                        load(to[:, :, :], weights[name][l].rearrange("t i o -> i t o"), s["w_kvq"])
                    sp.wait_ge(s["built"], 2)
                    with nc.allow_non_contiguous_dma(reason="small weights, once"):
                        for i, name in enumerate(("Watt", "Wmsg")):
                            for hd in range(H):
                                load(bd[i][hd * HS:(hd + 1) * HS, :, hd * HS:(hd + 1) * HS],
                                     weights[name][l, hd].rearrange("r i o -> i r o"), s["bd"])
                        for hd in range(H):
                            load(pri[hd * HS:(hd + 1) * HS, :], weights["pri"][l, hd:hd + 1, :].to_broadcast([HS, R]), s["bd"])
                    sp.wait_ge(s["dv"], h_at[0])
                    load(tiles(scratch["h"]), h[:, :, :], s["h_out"])

                    def put_q(t, u):
                        sp.wait_ge(s["qkv_sb"], t + 1)
                        sp.dma_start(scratch["q"][bass.ds(t * P, P), :], q_sb[u][:, :]).then_inc(q_out[u], 16)

                    with sp.Fori(0, NT // 2) as i:
                        for u in range(2):
                            put_q(i * 2 + u, u)
                    sp.wait_ge(s["h_out"], 16)
                    for u in range(2):
                        sp.wait_ge(q_out[u], 8 * NT)

            @block.scalar
            def _(act):
                a = nc.scalar
                if not first:
                    act.wait_ge(s["prod"], 2 * NT)
                    a.activation(h[:, :, :], h[:, :, :], ACT.Silu).then_inc(s["act"], 1)
                    act.wait_ge(s["dv"], sqrt_at[0])
                    a.activation(al[:, :], al[:, :], ACT.Sigmoid).then_inc(s["act"], 1)
                act.wait_ge(s["dv"], sqrt_at[-1])
                a.activation(st2[:, :], st2[:, :], ACT.Sqrt).then_inc(s["act"], 1)
                if last:
                    def turned(t, u):
                        act.wait_ge(s["tp"], t + 1)
                        a.activation(ht[u][:, 0, :], ps_a[:, u * 4, :], ACT.Copy).then_inc(s["ht"], 1)

                    with act.Fori(0, NT // 2) as i:
                        for u in range(2):
                            turned(i * 2 + u, u)
                    return

                def turned(t, u):
                    act.wait_ge(s["tp"], t + 1)
                    a.activation(ht[u][:, :, :], ps_a[:, :, :], ACT.Copy).then_inc(s["ht"], 1)

                def take(i, u, peeled=False):
                    t = i * 2 + u
                    act.wait_ge(s["qkv"], t + 1)
                    if not peeled:
                        act.wait_ge(q_out[u], i * 16)
                    a.activation(q_sb[u][:, :], ps_b[:, 1, 0:D], ACT.Copy).then_inc(s["qkv_sb"], 1)
                    if not peeled:
                        act.wait_ge(put_out[u], i * 16)
                    act.wait_ge(s["rel"], t * 2 + 1)
                    a.activation(kv[u][:, :, 0, :], ps_c[:, :, :], ACT.Copy).then_inc(s["rel_a"], 1)

                turned(0, 0)
                turned(1, 1)
                take(0, 0, True)
                turned(2, 0)
                take(0, 1, True)
                turned(3, 1)
                with act.Fori(1, NT // 2 - 1) as i:
                    for u in range(2):
                        take(i, u)
                        turned(i * 2 + u + 2, u)
                take(NT // 2 - 1, 0)
                take(NT // 2 - 1, 1)

            @block.tensor
            def _(pe):
                t_ = nc.tensor
                if not first:
                    pe.wait_ge(s["w"], 64)

                    def typed_out(t, u, peeled):
                        pe.wait_ge(s["agg"], t + 1)
                        if not peeled:
                            pe.wait_ge(s["prod"], t * 2 - 3)
                        ps = (ps_a, ps_c)[u]
                        for q in range(2):
                            ins = t_.matmul(ps[:, q * 4:(q + 1) * 4, :].rearrange("p a b -> p (a b)"), agg[u][:, :],
                                            wa[:, q * 4:(q + 1) * 4, :].rearrange("p a b -> p (a b)"), start=True, stop=True)
                        ins.then_inc(s["lin"], 1)

                    typed_out(0, 0, True)
                    typed_out(1, 1, True)
                    with pe.Fori(1, NT // 2) as i:
                        for u in range(2):
                            typed_out(i * 2 + u, u, False)
                if last:
                    pe.wait_ge(s["w_ff"], 32)

                    def turn(t, u, peeled):
                        pe.wait_ge(s["hm"], t + 1)
                        t_.transpose(ps_a[:, u * 4, :], hm[u][:, 0, :], c["ident"][:, :]).then_inc(s["tp"], 1)

                    def project(t, u, peeled):
                        pe.wait_ge(s["ht"], t + 1)
                        t_.matmul((ps_c, ps_d)[u][:, 0, 0:D], ht[u][:, 0, :], wff[:, :], start=True, stop=True).then_inc(s["qkv"], 1)

                    turn(0, 0, True)
                    turn(1, 1, True)
                    with pe.Fori(0, NT // 2 - 1) as i:
                        for u in range(2):
                            project(i * 2 + u, u, False)
                            turn(i * 2 + u + 2, u, False)
                    project(NT - 2, 0, False)
                    project(NT - 1, 1, False)
                    return
                pe.wait_ge(s["w_kvq"], 48)
                if not first:
                    pe.wait_ge(s["prod"], 2 * NT)

                def turn(t, u, peeled):
                    pe.wait_ge(s["hm"], t + 1)
                    if not peeled:
                        pe.wait_ge(s["ht"], t)
                    for k in range(TN):
                        ins = t_.transpose(ps_a[:, k, :], hm[u][:, k, :], c["ident"][:, :])
                    ins.then_inc(s["tp"], 1)

                def typed(t, u, peeled):
                    pe.wait_ge(s["ht"], t + 1)
                    if not peeled:
                        pe.wait_ge(s["rel_v"], t * 2 - 1)
                        pe.wait_ge(s["qkv_sb"], t)
                    for a, w in enumerate((wk, wv)):
                        for k in range(TN):
                            t_.matmul(ps_b[:, 0, a * P:(a + 1) * P], w[:, k, :], ht[u][:, k, :], start=k == 0, stop=k == TN - 1)
                    for k in range(TN):
                        ins = t_.matmul(ps_b[:, 1, 0:D], ht[u][:, k, :], wq[:, k, :], start=k == 0, stop=k == TN - 1)
                    ins.then_inc(s["qkv"], 1)

                def related(t, u, peeled):
                    pe.wait_ge(s["rel_v"], t * 2 + 1)
                    for a in range(2):
                        if not peeled:
                            pe.wait_ge(s[("rel_a", "rel_v")[a]], (t, t * 2)[a])
                        for q in range(2):
                            to = (ps_c[:, q * 4:(q + 1) * 4, :].rearrange("p a b -> p (a b)"), ps_d[:, q, :])[a]
                            ins = t_.matmul(to, kv_t[u][:, a, :], bd[a][:, q * 4:(q + 1) * 4, :].rearrange("p a b -> p (a b)"),
                                            start=True, stop=True)
                        ins.then_inc(s["rel"], 1)

                pe.wait_ge(s["dv"], bd_at[0])
                turn(0, 0, True)
                turn(1, 1, False)
                typed(0, 0, True)
                turn(2, 0, False)
                related(0, 0, True)
                typed(1, 1, False)
                turn(3, 1, False)
                related(1, 1, False)
                with pe.Fori(1, NT // 2 - 1) as i:
                    for u in range(2):
                        typed(i * 2 + u, u, False)
                        turn(i * 2 + u + 2, u, False)
                        related(i * 2 + u, u, False)
                for u in range(2):
                    typed(NT - 2 + u, u, False)
                    related(NT - 2 + u, u, False)

            @block.gpsimd
            def _(pool):
                g = nc.gpsimd
                if first:
                    pool.wait_ge(s["dv"], 1)

                def put(i, u, peeled=False):
                    t = i * 2 + u
                    if not peeled:
                        pool.wait_ge(put_out[u], i * 16)
                    g.tensor_copy(ids[u][:, :], tab["id"][:, bass.ds(t, 1)]).then_inc(s["id"], 1)
                    pool.wait_ge(s["id"], t + 1)
                    pool.wait_ge(s["qkv_sb" if last else "rel_a"], t + 1)
                    if not last:
                        pool.wait_ge(s["rel_v"], t * 2 + 2)
                    pool.sem_inc(s["go"], 1)
                    if last:
                        g.indirect_dma_start(out=out[:, :], out_offset=bass.IndirectOffsetOnAxis(ap=ids[u][:, :], axis=0),
                                             in_=y[u][:, :], in_offset=None, bounds_check=N - 1, oob_is_err=False).then_inc(put_out[u], 16)
                    else:
                        g.indirect_dma_start(out=scratch["kv"].rearrange("(n r) d -> n (r d)", r=R),
                                             out_offset=bass.IndirectOffsetOnAxis(ap=ids[u][:, :], axis=0),
                                             in_=kv[u][:, :, :, :].rearrange("p r a d -> p (r a d)"), in_offset=None).then_inc(put_out[u], 16)

                put(0, 0, True)
                put(0, 1, True)
                with pool.Fori(1, NT // 2) as i:
                    for u in range(2):
                        put(i, u)
                for u in range(2):
                    pool.wait_ge(put_out[u], 8 * NT)


def edge_stage(nc, c, sem, l, tab, scratch, acc):
    s = Signals(sem, f"edges{l}")
    rows_in = [sem(f"edges{l}_rows_in{j}") for j in range(U)]
    q_in = [sem(f"edges{l}_q_in{u}") for u in range(2)]
    TP = G // 2
    FOUR = 4
    NF = -(-G // FOUR)
    fours = [range(FOUR * k, min(G, FOUR * (k + 1))) for k in range(NF)]
    with ExitStack() as st:
        sb = lambda n, sh, d=F32: st.enter_context(nc.sbuf_tensor(f"g{l}_{n}", sh, d))
        pb = lambda n, sh: st.enter_context(nc.psum_tensor(f"g{l}_{n}", sh, F32))
        ids = [sb(f"ids{j}", [P, G], I32) for j in range(U)]
        rows = [sb(f"rows{j}", [P, G, 2 * D]) for j in range(U)]
        qw = [sb(f"qw{u}", [P, G, D]) for u in range(2)]
        hot = [sb(f"hot{j}", [P, G, P]) for j in range(U)]
        hot_t = sb("hot_t", [P, G, P])
        score = sb("score", [P, G, H])
        fwd, top, m, shifted, exp_t = (sb(n, [GH, P]) for n in ("fwd", "top", "m", "shifted", "exp_t"))
        ends = sb("ends", [GH, 2, G])
        carry = [sb(f"carry{u}", [H, G + 1]) for u in range(2)]
        into, top1, delta, grown = (sb(n, [H, G]) for n in ("into", "top1", "delta", "grown"))
        into_x = sb("into_x", [H, G, H])
        seam = sb("seam", [GH, P + 1], BF16)
        scale = [sb(f"scale{u}", [P, G]) for u in range(2)]
        firsts = [sb(f"firsts{u}", [P, G, 2]) for u in range(2)]
        ps_q = [pb(f"ps_q{u}", [P, FOUR, D]) for u in range(2)]
        ps_hot = [pb(f"ps_hot{u}", [P, FOUR, P]) for u in range(2)]
        ps_sum = [pb(f"ps_sum{u}", [P, 2, 2, P]) for u in range(2)]
        for_dve, for_act = pb("ps_dve", [P, 512]), pb("ps_act", [P, 512])
        score_t, ends_ps, into_ps = for_dve[0:GH, 0:P], for_dve[0:H, 128:128 + 2 * G], for_dve[0:GH, 160:161]
        exp_ps, scale_ps = for_act[:, 0:GH], for_act[:, 128:128 + G]

        def over(engine, body, after, count=B):
            for j in range(U):
                body(0, j, j)
            with engine.Fori(1, count // U) as i:
                for j in range(U):
                    body(i, j, i * U + j)
            if after:
                after()

        def in_flight(i, j, b):
            whole = isinstance(b, int)
            return tuple(None if whole and not 0 <= b - n < B else (b - n, (j - n) % U) for n in range(3))

        def early(b, n):
            return isinstance(b, int) and b < n

        def windows(engine, regs, b, g):
            if g % 4 == 0:
                engine.reg_load(regs, tab["w0"][0:1, bass.ds(b * NB + g, 4)])
            return engine.snap(regs[g % 4], min_val=0, max_val=N)

        with nc.Block() as block:
            @block.sync
            def _(sp):
                regs = [sp.alloc_register(f"sp_window{l}_{k}") for k in range(4)]

                def batch(i, j, b):
                    u = j % 2
                    if not early(b, 2):
                        sp.wait_ge(s["spread"], (b - 1) * NF)
                    for g in range(G):
                        w = windows(sp, regs, b, g)
                        sp.dma_start(qw[u][:, g, :], scratch["q"][bass.ds(w, P), :]).then_inc(q_in[u], 16)

                over(sp, batch, None)

            @block.gpsimd
            def _(pool):
                g_ = nc.gpsimd

                def batch(i, j, b):
                    if not early(b, U):
                        pool.wait_ge(s["sums"], (b - U + 1) * TP)
                    g_.tensor_copy(ids[j][:, :], tab["key"][:, bass.ds(b * G, G)]).then_inc(s["ids"], 1)
                    pool.wait_ge(s["ids"], b + 1)
                    pool.sem_inc(s["go"], 1)
                    for g in range(G):
                        g_.indirect_dma_start(out=rows[j][:, g, :], out_offset=None, in_=scratch["kv"][:, :],
                                              in_offset=bass.IndirectOffsetOnAxis(ap=ids[j][:, g:g + 1], axis=0)).then_inc(rows_in[j], 16)
                    if isinstance(b, int) and b == 0:
                        g_.memset(acc[:, :, :], 0.0).then_inc(s["zeroed"], 1)
                        for u in range(2):
                            g_.memset(carry[u][:, :], -BIG).then_inc(s["zeroed"], 1)

                over(pool, batch, None)

            @block.vector
            def _(dve):
                v = nc.vector
                regs = [dve.alloc_register(f"dve_window{l}_{k}") for k in range(4)]

                def one_hot(b, j):
                    if not early(b, U):
                        dve.wait_ge(s["sums"], (b - U + 1) * TP)
                    v.tensor_tensor(hot[j][:, :, :], c["row"][:, :].rearrange("p (o e) -> p o e", o=1).to_broadcast([P, G, P]),
                                    tab["rank"][:, bass.ds(b * G, G)].rearrange("p (g o) -> p g o", o=1).to_broadcast([P, G, P]),
                                    ALU.is_equal).then_inc(s["hot"], 1)

                def columns(b, j, some):
                    for g in some:
                        w = windows(dve, regs, b, g)
                        if g % 2 == 0:
                            dve.wait_ge(s["firsts"], b * TP + g // 2 + 1)
                        if not (early(b, 1) and g == 0):
                            dve.wait_ge(s["copied"], b * G + g)
                            dve.wait_ge(s["column"], b * G + g)
                        at = acc[:, :, bass.ds(w, 1)]
                        v.scalar_tensor_tensor(out=at, in0=at, scalar=scale[j % 2][:, g:g + 1], in1=firsts[j % 2][:, g, :].rearrange("p (a o) -> p a o", o=1),
                                               op0=ALU.mult, op1=ALU.add).then_inc(s["column"], 1)

                def products(i, j, b, some):
                    for k in some:
                        four = fours[k]
                        if k == 0:
                            dve.wait_ge(rows_in[j], (i + 1) * 16 * G)
                        part = rows[j][:, four[0]:four[-1] + 1, 0:D]
                        dve.wait_ge(s["spread"], b * NF + k + 1)
                        v.tensor_tensor(part, part, ps_q[k % 2][:, 0:len(four), :], ALU.mult).then_inc(s["prod"], 1)

                def scores(j, b):
                    for k in range(2):
                        dve.wait_ge(s["prod"], b * NF + (k + 1) * NF // 2)
                        v.reduce_sum(score[:, k * TP:(k + 1) * TP, :],
                                     rows[j][:, k * TP:(k + 1) * TP, 0:D].rearrange("p g (h d) -> p g h d", h=H),
                                     axis=AX.X).then_inc(s["score"], 1)

                def own_maxima(b):
                    dve.wait_ge(s["score_t"], b + 1)
                    dve.wait_ge(s["seam"], b + 1)
                    v.tensor_tensor_scan(fwd[:, :], seam[:, 0:P], score_t, -BIG, ALU.add, ALU.max).then_inc(s["chain"], 1)
                    dve.wait_ge(s["chain"], b * CHAIN + 1)
                    v.tensor_tensor_scan(top[:, ::-1], seam[:, 1:P + 1][:, ::-1], fwd[:, ::-1], -BIG, ALU.add, ALU.max).then_inc(s["chain"], 1)
                    dve.wait_ge(s["chain"], b * CHAIN + 2)
                    v.tensor_scalar(ends[:, 0, :], c["tile_mask"][:, :], top[:, 0:1], None, ALU.mult).then_inc(s["ends"], 1)
                    v.tensor_scalar(ends[:, 1, :], c["tile_mask"][:, :], top[:, P - 1:P], None, ALU.mult).then_inc(s["ends"], 1)

                def carried(b, j):
                    if early(b, 1):
                        dve.wait_ge(s["zeroed"], 3)
                    dve.wait_ge(s["ends_ps"], b + 1)
                    ca, cb = carry[j % 2], carry[1 - j % 2]
                    v.tensor_copy(ca[:, 0:1], cb[:, G:G + 1]).then_inc(s["chain"], 1)
                    v.tensor_tensor_scan(ca[:, 1:G + 1], tab["pass"][:, bass.ds(b * G, G)], ends_ps[:, G:2 * G],
                                         cb[:, G:G + 1], ALU.add, ALU.max).then_inc(s["chain"], 1)
                    dve.wait_ge(s["chain"], b * CHAIN + 4)
                    v.tensor_tensor(into[:, :], ca[:, 0:G], tab["new"][:, bass.ds(b * G, G)], ALU.add).then_inc(s["chain"], 1)
                    dve.wait_ge(s["chain"], b * CHAIN + 5)
                    v.tensor_tensor(top1[:, :], into[:, :], ends_ps[:, 0:G], ALU.max).then_inc(s["chain"], 1)
                    v.tensor_tensor(into_x[:, :, :], into[:, :].rearrange("p (g o) -> p g o", o=1).to_broadcast([H, G, H]),
                                    c["ident"][0:H, 0:H].rearrange("p (o h) -> p o h", o=1).to_broadcast([H, G, H]),
                                    ALU.mult).then_inc(s["carry"], 1)
                    dve.wait_ge(s["chain"], b * CHAIN + 6)
                    v.tensor_tensor(delta[:, :], into[:, :], top1[:, :], ALU.subtract).then_inc(s["scale"], 1)

                def shift(b):
                    dve.wait_ge(s["carry_ps"], b + 1)
                    v.scalar_tensor_tensor(out=m[:, :], in0=tab["first"][:, bass.ds(b, 1), :].rearrange("p o e -> p (o e)"),
                                           scalar=into_ps, in1=top[:, :], op0=ALU.add, op1=ALU.max).then_inc(s["chain"], 1)
                    dve.wait_ge(s["chain"], b * CHAIN + 7)
                    v.tensor_tensor(shifted[:, :], score_t, m[:, :], ALU.subtract).then_inc(s["shifted"], 1)

                def messages(b, j):
                    dve.wait_ge(s["exp_sb"], b + 1)
                    for k in range(2):
                        half = rows[j][:, k * TP:(k + 1) * TP, :]
                        v.tensor_tensor(half[:, :, D:2 * D], half[:, :, D:2 * D], half[:, :, 0:D], ALU.mult).then_inc(s["message"], 1)

                def step(i, j, b):
                    new, mid, old = in_flight(i, j, b)
                    if mid:
                        own_maxima(mid[0])
                    if new:
                        products(i, j, b, [0])
                    if mid:
                        carried(*mid)
                    if new and in_flight(i, j + 1, b + 1)[0]:
                        one_hot(b + 1, (j + 1) % U)
                    if mid:
                        shift(mid[0])
                    if new:
                        products(i, j, b, [1])
                    if old:
                        columns(*old, range(0, 4))
                    if new:
                        products(i, j, b, [2])
                    if old:
                        columns(*old, range(4, 8))
                    if new:
                        products(i, j, b, [3])
                        scores(j, b)
                    if mid:
                        messages(*mid)
                    if old:
                        columns(*old, range(8, G))

                one_hot(0, 0)

                def end():
                    for n in range(U + 2):
                        step(B // U - 1, n, B - U + n)

                over(dve, step, end, B - U)
                dve.wait_ge(s["column"], T)

            @block.scalar
            def _(act):
                a = nc.scalar
                regs = [act.alloc_register(f"act_window{l}_{k}") for k in range(4)]

                def copies(b, j, some):
                    for g in some:
                        w = windows(act, regs, b, g)
                        ps = ps_sum[(j * TP + g // 2) % 2]
                        if g % 2 == 0:
                            act.wait_ge(s["sums"], b * TP + g // 2 + 1)
                            a.activation(firsts[j % 2][:, g:g + 2, :].rearrange("p g (a o) -> p g a o", o=1),
                                         ps[:, :, :, 0:1], ACT.Copy).then_inc(s["firsts"], 1)
                        if early(b, 1) and g == 0:
                            act.wait_ge(s["zeroed"], 3)
                        else:
                            act.wait_ge(s["copied"], b * G + g)
                        a.activation(acc[:, :, bass.ds(w + 1, P - 1)], ps[:, g % 2, :, 1:P],
                                     ACT.Copy).then_inc(s["copied"], 1)

                def turned(b, some):
                    for k in some:
                        four = fours[k]
                        act.wait_ge(s["turned_ps"], b * NF + k + 1)
                        a.activation(hot_t[:, four[0]:four[-1] + 1, :], ps_hot[k % 2][:, 0:len(four), :], ACT.Copy).then_inc(s["turned"], 1)

                def flags(b):
                    if not early(b, 1):
                        act.wait_ge(s["chain"], b * CHAIN - CHAIN + 2)
                    a.activation(seam[:, :], tab["seam"][:, bass.ds(b, 1), :].rearrange("p o e -> p (o e)"),
                                 ACT.Copy).then_inc(s["seam"], 1)

                def step(i, j, b):
                    new, mid, old = in_flight(i, j, b)
                    if new:
                        turned(b, range(0, 3))
                    if old:
                        copies(*old, range(0, 4))
                    if mid:
                        act.wait_ge(s["scale"], mid[0] + 1)
                        a.activation(grown[:, :], delta[:, :], ACT.Exp).then_inc(s["scale_sb"], 1)
                    if new:
                        turned(b, [3])
                    if old:
                        copies(*old, range(4, 8))
                    if mid:
                        act.wait_ge(s["scale_ps"], mid[0] + 1)
                        a.activation(scale[mid[1] % 2][:, :], scale_ps, ACT.Copy).then_inc(s["scale_sb"], 1)
                        act.wait_ge(s["shifted"], mid[0] + 1)
                        a.activation(exp_t[:, :], shifted[:, :], ACT.Exp).then_inc(s["exp_t"], 1)
                    if old:
                        copies(*old, range(8, 10))
                    if mid:
                        act.wait_ge(s["exp_ps"], mid[0] + 1)
                        a.activation(rows[mid[1]][:, :, 0:D].rearrange("p g (h d) -> p g h d", h=H),
                                     exp_ps.rearrange("p (g h o) -> p g h o", h=H, o=1).to_broadcast([P, G, H, HS]), ACT.Copy).then_inc(s["exp_sb"], 1)
                    if old:
                        copies(*old, range(10, G))
                    if new:
                        flags(b)

                def end():
                    for n in range(2):
                        step(B // U, n, B + n)

                over(act, step, end)

            @block.tensor
            def _(pe):
                t = nc.tensor

                def sums(b, j, some):
                    for g in some:
                        if g == 0:
                            pe.wait_ge(s["message"], b * 2 + 1)
                        if g == TP:
                            pe.wait_ge(s["message"], b * 2 + 2)
                        if g % 2 == 0 and not (early(b, 1) and g < 4):
                            pe.wait_ge(s["copied"], b * G + g - 2)
                        ps = ps_sum[(j * TP + g // 2) % 2]
                        t.matmul(ps[:, g % 2, 0, :], rows[j][:, g, D:2 * D], hot[j][:, g, :], start=True, stop=True)
                        ins = t.matmul(ps[:, g % 2, 1, :], rows[j][:, g, 0:D], hot[j][:, g, :], start=True, stop=True)
                        if g % 2:
                            ins.then_inc(s["sums"], 1)

                def turn(b, j, some):
                    for k in some:
                        if k == 0:
                            pe.wait_ge(s["hot"], b + 1)
                        if not (early(b, 1) and k < 2):
                            pe.wait_ge(s["turned"], b * NF + k - 1)
                        for n, g in enumerate(fours[k]):
                            ins = t.transpose(ps_hot[k % 2][:, n, :], hot[j][:, g, :], c["ident"][:, :])
                        ins.then_inc(s["turned_ps"], 1)

                def spread(i, j, b, some):
                    for k in some:
                        if k == 0:
                            pe.wait_ge(q_in[j % 2], (i * 2 + j // 2 + 1) * 16 * G)
                        pe.wait_ge(s["turned"], b * NF + k + 1)
                        if not (early(b, 1) and k < 2):
                            pe.wait_ge(s["prod"], b * NF + k - 1)
                        for n, g in enumerate(fours[k]):
                            ins = t.matmul(ps_q[k % 2][:, n, :], hot_t[:, g, :], qw[j % 2][:, g, :], start=True, stop=True)
                        ins.then_inc(s["spread"], 1)

                def step(i, j, b):
                    new, mid, old = in_flight(i, j, b)
                    if new:
                        turn(b, j, [0, 1])
                    if mid:
                        pe.wait_ge(s["score"], mid[0] * 2 + 2)
                        t.transpose(score_t, score[:, :, :].rearrange("p g h -> p (g h)"), c["ident"][:, :]).then_inc(s["score_t"], 1)
                    if new:
                        spread(i, j, b, [0])
                        turn(b, j, [2])
                    if old:
                        sums(*old, range(0, 4))
                    if mid:
                        pe.wait_ge(s["ends"], mid[0] * 2 + 2)
                        t.matmul(ends_ps, c["head_of_row"][:, :], ends[:, :, :].rearrange("p a g -> p (a g)"), start=True, stop=True).then_inc(s["ends_ps"], 1)
                    if new:
                        turn(b, j, [3])
                        spread(i, j, b, [1])
                    if old:
                        sums(*old, range(4, 8))
                    if mid:
                        pe.wait_ge(s["carry"], mid[0] + 1)
                        t.matmul(into_ps, into_x[:, :, :].rearrange("p g h -> p (g h)"), c["ones"][0:H, 0:1], start=True, stop=True).then_inc(s["carry_ps"], 1)
                        pe.wait_ge(s["scale_sb"], mid[0] * 2 + 1)
                        t.matmul(scale_ps, c["head_of_feature"][:, :], grown[:, :], start=True, stop=True).then_inc(s["scale_ps"], 1)
                    if new:
                        spread(i, j, b, [2])
                    if old:
                        sums(*old, range(8, 10))
                    if new:
                        spread(i, j, b, [3])
                    if mid:
                        pe.wait_ge(s["exp_t"], mid[0] + 1)
                        t.transpose(exp_ps, exp_t[:, :], c["ident"][0:GH, 0:GH]).then_inc(s["exp_ps"], 1)
                    if old:
                        sums(*old, range(10, G))

                def end():
                    for n in range(2):
                        step(B // U, n, B + n)

                over(pe, step, end)


CHAIN = 7


def gnn(nc: bass.Bass, x, src, dst, edge_type_8, node_type_8, Wk, Wq, Wv, Wa, pri, Watt, Wmsg, skip, ln_g, ln_b,
        Wff, bff, out):
    weights = dict(Wk=Wk, Wq=Wq, Wv=Wv, Wa=Wa, pri=pri, Watt=Watt, Wmsg=Wmsg, skip=skip, ln_g=ln_g, ln_b=ln_b,
                   Wff=Wff, bff=bff)
    dram = lambda n, sh, d=F32: nc.dram_tensor(n, sh, d, kind="Internal").ap()
    edge_dst, edge_key = dram("edge_dst", [EP + 1], I32), dram("edge_key", [EP], I32)
    scratch = dict(w0=dram("window_starts", [B * NB], I32), rank=dram("edge_rank", [EP]), new=dram("tile_new", [T], BF16),
                   pas=dram("tile_pass", [T], BF16), rows=dram("node_rows", [NP, XW]), h=dram("node_h", [NP, D]),
                   q=dram("node_q", [NP, D]), kv=dram("node_kv", [NP * R, 2 * D]))
    with ExitStack() as st:
        sb = lambda n, s, d=F32: st.enter_context(nc.sbuf_tensor(n, s, d))
        sem = lambda n: st.enter_context(nc.semaphore(n))
        c = constants(nc, sb, sem)
        tab = dict(key=sb("edge_key_sb", [P, T], I32), rank=sb("edge_rank_sb", [P, T]),
                   first=sb("first_flags", [GH, B, P], BF16), seam=sb("seam_flags", [GH, B, P + 1], BF16),
                   w0=sb("window_starts_sb", [1, B * NB], I32), new=sb("tile_new_sb", [H, T], BF16),
                   id=sb("node_id", [P, NT], I32), type=sb("node_type", [P, NT, TN]))
        tab["pass"] = sb("tile_pass_sb", [H, T], BF16)
        unsorted = sb("unsorted", [1, 1], I32)
        edge_lists(nc, sem, dst, src, edge_type_8, edge_dst, edge_key, unsorted)
        edge_sort(nc, c, sem, edge_dst, edge_key, unsorted, dram("dst_slots", [NP, 1]))
        edge_tables(nc, c, sem, x, node_type_8, edge_dst, edge_key, tab, scratch)
        acc = sb("acc", [P, 2, NP])
        for l in range(L):
            node_stage(nc, c, sem, l, tab, scratch, acc, weights, out)
            edge_stage(nc, c, sem, l, tab, scratch, acc)
        node_stage(nc, c, sem, L, tab, scratch, acc, weights, out)


_INS = ["x", "src", "dst", "edge_type_8", "node_type_8"] + ["L0_gnn_" + n for n in (
    "Wk", "Wq", "Wv", "Wa", "pri", "Watt", "Wmsg", "skip", "ln_g", "ln_b", "Wff", "bff")]


def kernel(**inputs):
    import numpy as _np
    import concourse.bacc as _bacc
    from concourse.bass_utils import run_bass_kernel_spmd as _run

    nc = _bacc.Bacc("TRN2", target_bir_lowering=False, num_devices=1)
    arrays, args = {}, []
    for name in _INS:
        a = _np.ascontiguousarray(inputs[name])
        arrays[f"in_{name}"] = a
        args.append(nc.dram_tensor(f"in_{name}", a.shape, mybir.dt.from_np(a.dtype), kind="ExternalInput").ap())
    out = nc.dram_tensor("out_nodes", (N, D), F32, kind="ExternalOutput").ap()
    gnn(nc, *args, out)
    r = _run(nc, [arrays], core_ids=[0])
    return r.results[0]["out_nodes"]
```

```python
import concourse.bass as bass
from concourse import mybir
from contextlib import ExitStack

F32 = mybir.dt.float32
BF16 = mybir.dt.bfloat16
I32 = mybir.dt.int32
ALU = mybir.AluOpType
ACT = mybir.ActivationFunctionType
AX = mybir.AxisListType

P = 128
N = 6250
E = 100000
D = 128
H = 8
HS = D // H
TN = 8
R = 8
L = 2
NT = 50
NP = NT * P
G = 14
GH = G * H
B = 56
U = 4
T = B * G
EP = T * P
Q = 112
K7 = T // Q
W = K7 * P
NB = 16
BIG = 1e30
EPS = 1e-5
XW = D + 2


class Signals(dict):

    def __init__(self, sem, stage):
        self.sem, self.stage = sem, stage

    def __missing__(self, name):
        self[name] = self.sem(f"{self.stage}_{name}")
        return self[name]

    def clear(self, engine):
        for x in self.values():
            engine.sem_clear(x)


def constants(nc, sb, sem):
    c = {}
    c["ident"] = sb("ident", [P, P])
    c["row"] = sb("row_iota", [P, P])
    c["before"] = sb("before", [P, P])
    c["ones"] = sb("ones", [P, P])
    c["tile_mask"] = sb("tile_mask", [GH, G])
    c["head_of_row"] = sb("head_of_row", [GH, H])
    c["head_of_feature"] = sb("head_of_feature", [H, D])
    c["type_iota"] = sb("type_iota", [P, TN])
    c["type_iota_i"] = sb("type_iota_i", [P, P], I32)
    made, copied = sem("constants_made"), sem("constants_copied")
    with nc.Block() as block:
        @block.gpsimd
        def _(pool):
            g = nc.gpsimd
            g.memset(c["ones"][:, :], 1.0).then_inc(made, 1)
            g.iota(c["type_iota_i"][:, :], [[1, P]], base=0, channel_multiplier=0).then_inc(made, 1)
            pool.wait_ge(made, 2)
            one = c["ones"]
            g.affine_select(out=c["ident"][:, :], in_=one[:, :], compare_op=ALU.is_equal, fill=0.0, base=0,
                            pattern=[[1, P]], channel_multiplier=-1).then_inc(made, 1)
            g.affine_select(out=c["before"][:, :], in_=one[:, :], compare_op=ALU.is_ge, fill=0.0, base=-1,
                            pattern=[[1, P]], channel_multiplier=-1).then_inc(made, 1)
            g.affine_select(out=c["head_of_feature"][:, :], in_=one[0:H, :], compare_op=ALU.is_ge, fill=0.0,
                            base=0, pattern=[[1, D]], channel_multiplier=-HS).then_inc(made, 1)
            g.affine_select(out=c["tile_mask"][:, :], in_=one[0:GH, 0:G], compare_op=ALU.is_ge, fill=0.0,
                            base=0, pattern=[[-H, G]], channel_multiplier=1).then_inc(made, 1)
            pool.wait_ge(made, 6)
            g.affine_select(out=c["head_of_feature"][:, :], in_=c["head_of_feature"][:, :], compare_op=ALU.is_ge,
                            fill=0.0, base=HS - 1, pattern=[[-1, D]], channel_multiplier=HS).then_inc(made, 1)
            g.affine_select(out=c["tile_mask"][:, :], in_=c["tile_mask"][:, :], compare_op=ALU.is_ge,
                            fill=0.0, base=H - 1, pattern=[[H, G]], channel_multiplier=-1).then_inc(made, 1)

        @block.vector
        def _(dve):
            dve.wait_ge(made, 8)
            nc.vector.tensor_copy(c["row"][:, :], c["type_iota_i"][:, :]).then_inc(copied, 1)
            nc.vector.tensor_copy(c["type_iota"][:, :], c["type_iota_i"][:, 0:TN]).then_inc(copied, 1)
            nc.vector.tensor_reduce(c["head_of_row"][:, :],
                                    c["ident"][0:GH, 0:GH].rearrange("p (g h) -> p h g", h=H),
                                    axis=AX.X, op=ALU.add).then_inc(copied, 1)
    return c


def edge_lists(nc, sem, dst, src, etype, edge_dst, edge_key, unsorted):
    full = E // W
    rest = E - full * W
    loaded, filled, keyed, stored, counted, summed = (sem(f"lists_{x}") for x in (
        "loaded", "filled", "keyed", "stored", "counted", "summed"))
    with ExitStack() as st:
        sb = lambda n, s, d=F32: st.enter_context(nc.sbuf_tensor(n, s, d))
        dsts, srcs, rels, prev = (sb(f"l_{x}", [Q, W], I32) for x in ("dst", "src", "rel", "prev"))
        lead = sb("l_lead", [1, 1], I32)
        falls, count, one = sb("l_falls", [Q, W]), sb("l_count", [Q, 1]), sb("l_one", [Q, 1])
        ps = st.enter_context(nc.psum_tensor("l_ps", [1, 1], F32))
        with nc.Block() as block:
            @block.sync
            def _(sp):
                sp.wait_ge(filled, 4)
                for to, of in ((dsts, dst), (srcs, src), (rels, etype)):
                    sp.dma_start(to[0:full, :], of[0:full * W].rearrange("(p w) -> p w", w=W)).then_inc(loaded, 16)
                    sp.dma_start(to[full:full + 1, 0:rest], of[full * W:E].rearrange("(p w) -> p w", p=1)).then_inc(loaded, 16)
                sp.wait_ge(loaded, 96)
                sp.dma_start(edge_dst[1:EP + 1].rearrange("(p w) -> p w", w=W), dsts[:, :]).then_inc(stored, 16)
                sp.dma_start(edge_dst[0:1].rearrange("(p w) -> p w", p=1), lead[:, :]).then_inc(stored, 16)
                sp.wait_ge(keyed, 1)
                sp.dma_start(edge_key.rearrange("(p w) -> p w", w=W), srcs[:, :]).then_inc(stored, 16)
                sp.wait_ge(stored, 48)
                sp.dma_start(prev[:, :], edge_dst[0:EP].rearrange("(p w) -> p w", w=W)).then_inc(loaded, 16)

            @block.vector
            def _(dve):
                v = nc.vector
                v.memset(dsts[:, :], N).then_inc(filled, 1)
                v.memset(srcs[:, :], 0).then_inc(filled, 1)
                v.memset(rels[:, :], 0).then_inc(filled, 1)
                v.memset(lead[:, :], -1).then_inc(filled, 1)
                v.memset(one[:, :], 1.0).then_inc(filled, 1)
                dve.wait_ge(loaded, 96)
                v.scalar_tensor_tensor(out=srcs[:, :], in0=srcs[:, :], scalar=float(R), in1=rels[:, :],
                                       op0=ALU.mult, op1=ALU.add).then_inc(keyed, 1)
                dve.wait_ge(loaded, 112)
                v.tensor_tensor(falls[:, :], prev[:, :], dsts[:, :], ALU.is_gt).then_inc(counted, 1)
                dve.wait_ge(counted, 1)
                v.reduce_sum(count[:, :], falls[:, :], axis=AX.X).then_inc(counted, 1)
                dve.wait_ge(summed, 1)
                v.tensor_copy(unsorted[:, :], ps[:, :]).then_inc(counted, 1)

            @block.tensor
            def _(pe):
                pe.wait_ge(filled, 5)
                pe.wait_ge(counted, 2)
                nc.tensor.matmul(ps[:, :], count[:, :], one[:, :], start=True, stop=True).then_inc(summed, 1)


def edge_sort(nc, c, sem, edge_dst, edge_key, unsorted, slots):
    s = Signals(sem, "sort")
    C1, C2 = 10, 6
    with ExitStack() as st:
        sb = lambda n, sh, d=F32: st.enter_context(nc.sbuf_tensor(f"s_{n}", sh, d))
        dst, key = sb("dst", [P, T], I32), sb("key", [P, T], I32)
        dstf, number = sb("dstf", [P, T]), sb("number", [P, T])
        after, diag, same = sb("after", [P, P]), sb("diag", [P, P]), sb("same", [P, P])
        zero, count, run = sb("zero", [P, NT]), sb("count", [P, NT]), sb("run", [P, NT])
        col, rank, total, held, place = (sb(n, [P, 1]) for n in ("col", "rank", "total", "held", "place"))
        idx, key_c, to, to1 = (sb(n, [P, 1], I32) for n in ("idx", "key_c", "to", "to1"))
        ps = st.enter_context(nc.psum_tensor("s_ps", [P, P], F32))
        ps1 = st.enter_context(nc.psum_tensor("s_ps1", [P, 1], F32))
        by_edge = lambda a: a.rearrange("(p t) -> p t", t=T)
        by_node = slots.rearrange("(p t) o -> p (t o)", t=NT)

        def where_unsorted(engine):
            flag = engine.alloc_register("unsorted")
            engine.reg_load(flag, unsorted[0:1, 0:1])
            return engine.If(engine.snap(flag, min_val=0, max_val=EP) > 0)

        with nc.Block() as block:
            @block.sync
            def _(sp):
                with where_unsorted(sp):
                    sp.dma_start(dst[:, :], by_edge(edge_dst[1:EP + 1])).then_inc(s["loaded"], 16)
                    sp.dma_start(key[:, :], by_edge(edge_key)).then_inc(s["loaded"], 16)
                    sp.wait_ge(s["dv"], 1)
                    sp.dma_start(by_node, zero[:, :]).then_inc(s["slots"], 16)
                    sp.wait_ge(s["put"], 16 * T)
                    sp.dma_start(count[:, :], by_node).then_inc(s["loaded"], 16)
                    sp.wait_ge(s["dv"], 4 + T * C1 + 3)
                    sp.dma_start(by_node, run[:, :]).then_inc(s["slots"], 16)
                    sp.wait_ge(s["slots"], 32)

            @block.vector
            def _(dve):
                v = nc.vector

                def chain(at):
                    k = [0]

                    def then(ins, wait=True):
                        k[0] += 1
                        ins.then_inc(s["dv"], 1)
                        if wait:
                            dve.wait_ge(s["dv"], at + k[0])
                    return then

                with where_unsorted(dve):
                    then = chain(0)
                    then(v.memset(zero[:, :], 0.0))
                    then(v.tensor_tensor(after[:, :], c["ones"][:, :], c["before"][:, :], ALU.subtract))
                    then(v.tensor_tensor(after[:, :], after[:, :], c["ident"][:, :], ALU.subtract))
                    dve.wait_ge(s["loaded"], 32)
                    then(v.tensor_copy(dstf[:, :], dst[:, :]))
                    with dve.Fori(0, T) as t:
                        dve.wait_ge(s["go"], t * 3 + 1)
                        then = chain(t * C1 + 4)
                        then(v.tensor_copy(col[:, :], dstf[:, bass.ds(t, 1)]))
                        then(v.tensor_copy(idx[:, :], dst[:, bass.ds(t, 1)]))
                        then(v.tensor_scalar(diag[:, :], c["ident"][:, :], col[:, 0:1], None, ALU.mult))
                        dve.wait_ge(s["pe"], t + 1)
                        then(v.tensor_scalar(same[:, :], ps[:, :], col[:, 0:1], None, ALU.is_equal))
                        then(v.reduce_sum(total[:, :], same[:, :], axis=AX.X))
                        then(v.tensor_tensor(same[:, :], same[:, :], after[:, :], ALU.mult))
                        then(v.reduce_sum(rank[:, :], same[:, :], axis=AX.X))
                        dve.wait_ge(s["got"], (t + 1) * 16)
                        then(v.tensor_tensor(rank[:, :], rank[:, :], held[:, :], ALU.add))
                        then(v.tensor_copy(number[:, bass.ds(t, 1)], rank[:, :]))
                        then(v.tensor_tensor(total[:, :], total[:, :], held[:, :], ALU.add), wait=False)
                    then = chain(4 + T * C1)
                    dve.wait_ge(s["loaded"], 48)
                    then(v.tensor_tensor_scan(run[:, :], count[:, :], count[:, :], 0.0, ALU.add, ALU.max))
                    dve.wait_ge(s["pe"], T + 1)
                    then(v.tensor_scalar(run[:, :], run[:, :], ps1[:, 0:1], None, ALU.add))
                    then(v.tensor_tensor(run[:, :], run[:, :], count[:, :], ALU.subtract))
                    with dve.Fori(0, T) as t:
                        dve.wait_ge(s["go"], (t + T) * 3 + 2)
                        then = chain(t * C2 + (4 + T * C1 + 3))
                        then(v.tensor_copy(idx[:, :], dst[:, bass.ds(t, 1)]))
                        then(v.tensor_copy(key_c[:, :], key[:, bass.ds(t, 1)]))
                        then(v.tensor_copy(rank[:, :], number[:, bass.ds(t, 1)]))
                        dve.wait_ge(s["got"], (t + T + 1) * 16)
                        then(v.tensor_tensor(place[:, :], held[:, :], rank[:, :], ALU.add))
                        then(v.tensor_copy(to[:, :], place[:, :]))
                        then(v.tensor_scalar(to1[:, :], place[:, :], 1.0, None, ALU.add), wait=False)
                    v.memset(zero[:, :], 0.0).then_inc(s["dv"], 1)

            @block.tensor
            def _(pe):
                with where_unsorted(pe):
                    with pe.Fori(0, T) as t:
                        pe.wait_ge(s["dv"], t * C1 + 7)
                        nc.tensor.matmul(ps[:, :], c["ones"][:, :], diag[:, :], start=True, stop=True).then_inc(s["pe"], 1)
                    pe.wait_ge(s["dv"], 4 + T * C1 + 1)
                    nc.tensor.matmul(ps1[:, :], c["before"][:, :], run[:, NT - 1:NT], start=True, stop=True).then_inc(s["pe"], 1)

            @block.gpsimd
            def _(pool):
                g = nc.gpsimd
                at = lambda ap: bass.IndirectOffsetOnAxis(ap=ap[:, 0:1], axis=0)

                def ready():
                    pool.sem_inc(s["go"], 1)

                with where_unsorted(pool):
                    pool.wait_ge(s["slots"], 16)
                    ready()
                    with pool.Fori(0, T) as t:
                        pool.wait_ge(s["dv"], t * C1 + 6)
                        ready()
                        g.indirect_dma_start(out=held[:, :], out_offset=None, in_=slots[:, :], in_offset=at(idx)).then_inc(s["got"], 16)
                        pool.wait_ge(s["dv"], t * C1 + (4 + C1))
                        ready()
                        g.indirect_dma_start(out=slots[:, :], out_offset=at(idx), in_=total[:, :], in_offset=None).then_inc(s["put"], 16)
                        pool.wait_ge(s["put"], (t + 1) * 16)
                        ready()
                    pool.wait_ge(s["slots"], 32)
                    ready()
                    with pool.Fori(0, T) as t:
                        pool.wait_ge(s["dv"], t * C2 + (4 + T * C1 + 4))
                        ready()
                        g.indirect_dma_start(out=held[:, :], out_offset=None, in_=slots[:, :], in_offset=at(idx)).then_inc(s["got"], 16)
                        pool.wait_ge(s["dv"], t * C2 + (4 + T * C1 + 3 + C2))
                        ready()
                        g.indirect_dma_start(out=edge_dst.rearrange("(e o) -> e o", o=1), out_offset=at(to1), in_=idx[:, :],
                                             in_offset=None).then_inc(s["put"], 16)
                        g.indirect_dma_start(out=edge_key.rearrange("(e o) -> e o", o=1), out_offset=at(to), in_=key_c[:, :],
                                             in_offset=None).then_inc(s["put"], 16)
                        pool.wait_ge(s["put"], (t * 2 + T + 2) * 16)
                        ready()
                    pool.wait_ge(s["put"], 16 * 3 * T)
                    ready()


def edge_tables(nc, c, sem, x, ntype, edge_dst, edge_key, tab, scratch):
    s = Signals(sem, "tables")
    with ExitStack() as st:
        sb = lambda n, sh, d=F32: st.enter_context(nc.sbuf_tensor(n, sh, d))
        cur, prev, key, lo_i, hi_i = (sb(f"e_{n}", [Q, W], I32) for n in ("cur", "prev", "key", "lo_i", "hi_i"))
        start, cid, rank, keyf, lo, hi = (sb(f"e_{n}", [Q, W]) for n in ("start", "cid", "rank", "keyf", "lo", "hi"))
        base, w0 = sb("e_base", [Q, 1]), sb("e_w0", [Q, K7])
        w0_i = sb("e_w0_i", [Q, K7], I32)
        new_f, pas_f = sb("e_new", [Q, K7], BF16), sb("e_pas", [Q, K7], BF16)
        lo_t, hi_t = sb("e_lo_t", [P, T], BF16), sb("e_hi_t", [P, T], BF16)
        row_b = sb("e_row_b", [P, P], BF16)
        hot_lo = [sb(f"e_hot_lo{u}", [P, G, P], BF16) for u in range(2)]
        hot_hi = [sb(f"e_hot_hi{u}", [P, G, NT], BF16) for u in range(2)]
        off_hi = [sb(f"e_off_hi{u}", [P, G, NT], BF16) for u in range(2)]
        zero_b = sb("e_zero_b", [P, P], BF16)
        has, pre, tot, run, num, cf = (sb(f"e_{n}", [P, NT]) for n in ("has", "pre", "tot", "run", "num", "cf"))
        nt_i, n_i, compact = sb("e_nt_i", [P, NT], I32), sb("e_n_i", [P, NT], I32), sb("e_compact", [P, NT], I32)
        lrb = sb("e_lrb", [GH, B, P])
        xr = sb("e_xr", [P, NT, XW])
        ps_t = [st.enter_context(nc.psum_tensor(f"e_ps_t{u}", [P, K7 + 1, P], F32)) for u in range(2)]
        ps_h = st.enter_context(nc.psum_tensor("e_ps_h", [P, NT], F32))
        ps_s = st.enter_context(nc.psum_tensor("e_ps_s", [P, 256], F32))
        full = N // P
        rest = N - full * P
        HALF = B // 2
        tiles_of = lambda a: a[:, :].rearrange("p (q k) -> p k q", k=K7)
        with nc.Block() as block:
            @block.sync
            def _(sp):
                sp.dma_start(cur[:, :], edge_dst[1:EP + 1].rearrange("(p w) -> p w", w=W)).then_inc(s["loaded"], 16)
                sp.dma_start(prev[:, :], edge_dst[0:EP].rearrange("(p w) -> p w", w=W)).then_inc(s["loaded"], 16)
                sp.dma_start(key[:, :], edge_key.rearrange("(p w) -> p w", w=W)).then_inc(s["loaded"], 16)
                sp.wait_ge(s["filled"], 2)
                sp.dma_start(xr[:, 0:full, 0:D], x[0:full * P, :].rearrange("(t p) d -> p t d", p=P)).then_inc(s["nodes_in"], 16)
                sp.dma_start(xr[0:rest, full, 0:D], x[full * P:N, :]).then_inc(s["nodes_in"], 16)
                with nc.allow_non_contiguous_dma(reason="one word for each node, once"):
                    sp.dma_start(nt_i[:, 0:full], ntype[0:full * P].rearrange("(t p) -> p t", p=P)).then_inc(s["nodes_in"], 16)
                    sp.dma_start(nt_i[0:rest, full:full + 1], ntype[full * P:N].rearrange("(p o) -> p o", o=1)).then_inc(s["nodes_in"], 16)
                sp.wait_ge(s["dv"], 12)
                w0_d = scratch["w0"].rearrange("(b s) -> b s", s=NB)
                with nc.allow_non_contiguous_dma(reason="a few words, once"):
                    sp.dma_start(w0_d[:, 0:K7], w0_i[0:Q:2, :]).then_inc(s["stored"], 16)
                    sp.dma_start(w0_d[:, K7:G], w0_i[1:Q:2, :]).then_inc(s["stored"], 16)
                    sp.dma_start(w0_d[:, G:NB], w0_i[0:Q:2, 0:NB - G]).then_inc(s["stored"], 16)
                sp.dma_start(scratch["rank"].rearrange("(p w) -> p w", w=W), rank[:, :]).then_inc(s["stored"], 16)
                sp.dma_start(scratch["new"].rearrange("(p w) -> p w", w=K7), new_f[:, :]).then_inc(s["stored"], 16)
                sp.dma_start(scratch["pas"].rearrange("(p w) -> p w", w=K7), pas_f[:, :]).then_inc(s["stored"], 16)
                sp.wait_ge(s["stored"], 96)
                sp.dma_start(tab["w0"][:, :], scratch["w0"].rearrange("(p w) -> p w", p=1)).then_inc(s["rows_in"], 16)
                for to, of in ((tab["new"], scratch["new"]), (tab["pass"], scratch["pas"])):
                    sp.dma_start(to[:, :], of.rearrange("(p w) -> p w", p=1).to_broadcast([H, T])).then_inc(s["rows_in"], 16)
                rank_d = scratch["rank"].rearrange("(b g o e) -> g o b e", g=G, e=P, o=1)
                for g in range(G):
                    sp.dma_start(lrb[g * H:(g + 1) * H, :, :], rank_d[g].to_broadcast([H, B, P])).then_inc(s["lrb_in"], 16)
                sp.wait_ge(s["rows_in"], 48)

            @block.vector
            def _(dve):
                v = nc.vector
                n = [0]

                def did(ins):
                    ins.then_inc(s["dv"], 1)
                    n[0] += 1

                def then(ins):
                    did(ins)
                    dve.wait_ge(s["dv"], n[0])

                dve.wait_ge(s["loaded"], 48)
                did(v.tensor_tensor(start[:, :], cur[:, :], prev[:, :], ALU.not_equal))
                did(v.tensor_copy(keyf[:, :], key[:, :]))
                did(v.tensor_scalar(lo_i[:, :], cur[:, :], P - 1, None, ALU.bitwise_and))
                then(v.tensor_scalar(hi_i[:, :], cur[:, :], 7, None, ALU.arith_shift_right))
                did(v.tensor_copy(lo[:, :], lo_i[:, :]))
                did(v.tensor_copy(hi[:, :], hi_i[:, :]))
                then(v.tensor_tensor_scan(cid[:, :], start[:, :], start[:, :], 0.0, ALU.add, ALU.max))
                dve.wait_ge(s["pe"], 1)
                then(v.tensor_scalar(cid[:, :], cid[:, :], ps_s[0:Q, 0:1], -1.0, ALU.add, ALU.add))
                c3 = cid[:, :].rearrange("p (k e) -> p k e", e=P)
                r3 = rank[:, :].rearrange("p (k e) -> p k e", e=P)
                s3 = start[:, :].rearrange("p (k e) -> p k e", e=P)
                did(v.tensor_copy(w0_i[:, :], c3[:, :, 0]))
                then(v.tensor_tensor(r3, c3, c3[:, :, 0:1].to_broadcast([Q, K7, P]), ALU.subtract))
                then(v.tensor_scalar(new_f[:, :], s3[:, :, 0], -BIG, None, ALU.mult))
                did(v.scalar_tensor_tensor(out=pas_f[:, :], in0=r3[:, :, P - 1], scalar=-BIG, in1=new_f[:, :],
                                           op0=ALU.mult, op1=ALU.add))
                then(v.tensor_copy(row_b[:, :], c["row"][:, :]))
                dve.wait_ge(s["pe"], 2)
                did(v.tensor_copy(tiles_of(tab["rank"]), ps_t[0][:, 0:K7, 0:Q]))
                dve.wait_ge(s["pe"], 3)
                did(v.tensor_copy(tiles_of(tab["key"]), ps_t[1][:, 0:K7, 0:Q]))
                dve.wait_ge(s["pe"], 4)
                did(v.tensor_copy(tiles_of(lo_t), ps_t[0][:, 0:K7, 0:Q]))
                dve.wait_ge(s["pe"], 5)
                then(v.tensor_copy(tiles_of(hi_t), ps_t[1][:, 0:K7, 0:Q]))

                def hots(b, u, i):
                    if i is not None:
                        dve.wait_ge(s["counted"], b - 1)
                    v.tensor_tensor(hot_lo[u][:, :, :], row_b[:, :].rearrange("p (o e) -> p o e", o=1).to_broadcast([P, G, P]),
                                    lo_t[:, bass.ds(b * G, G)].rearrange("p (g o) -> p g o", o=1).to_broadcast([P, G, P]),
                                    ALU.is_equal).then_inc(s["hot"], 1)

                hots(0, 0, None)
                hots(1, 1, None)
                with dve.Fori(1, HALF) as i:
                    hots(i * 2, 0, i)
                    hots(i * 2 + 1, 1, i)
                dve.wait_ge(s["counted"], B + 1)
                then(v.tensor_scalar(has[:, :], ps_h[:, :], 1.0, None, ALU.min))
                dve.wait_ge(s["filled"], 4)
                did(v.tensor_copy(num[:, :], n_i[:, :]))
                dve.wait_ge(s["pe"], 6)
                did(v.tensor_copy(pre[:, :], ps_s[:, 64:64 + NT]))
                then(v.tensor_copy(tot[:, :], ps_s[:, 128:128 + NT]))
                then(v.tensor_tensor_scan(run[:, :], tot[:, :], tot[:, :], 0.0, ALU.add, ALU.max))
                then(v.tensor_tensor(pre[:, :], pre[:, :], run[:, :], ALU.add))
                then(v.tensor_tensor(pre[:, :], pre[:, :], tot[:, :], ALU.subtract))
                then(v.tensor_tensor(cf[:, :], num[:, :], pre[:, :], ALU.subtract))
                then(v.tensor_scalar(cf[:, :], cf[:, :], run[:, NT - 1:NT], None, ALU.add))
                then(v.tensor_tensor(pre[:, :], pre[:, :], cf[:, :], ALU.subtract))
                then(v.tensor_tensor(pre[:, :], pre[:, :], has[:, :], ALU.mult))
                then(v.tensor_tensor(compact[:, :], cf[:, :], pre[:, :], ALU.add))
                dve.wait_ge(s["nodes_in"], 64)
                did(v.tensor_copy(xr[:, :, D], nt_i[:, :]))
                did(v.tensor_copy(xr[:, :, D + 1], num[:, :]))
                dve.wait_ge(s["lrb_in"], 16 * G)
                then(v.memset(tab["seam"][:, :, :], 0.0))
                then(v.tensor_tensor(tab["seam"][:, :, 1:P], lrb[:, :, 1:P], lrb[:, :, 0:P - 1], ALU.subtract))
                did(v.tensor_scalar(tab["seam"][:, :, 1:P], tab["seam"][:, :, 1:P], -BIG, None, ALU.mult))

            @block.tensor
            def _(pe):
                t = nc.tensor
                pe.wait_ge(s["dv"], 7)
                t.matmul(ps_s[0:Q, 0:1], c["before"][0:Q, 0:Q], cid[:, W - 1:W], start=True, stop=True).then_inc(s["pe"], 1)
                for i, a in enumerate((rank, keyf, lo, hi)):
                    pe.wait_ge(s["dv"], (10, 10, 14, 15)[i])
                    for k in range(K7):
                        last = t.transpose(ps_t[i % 2][:, k, 0:Q], a[:, k * P:(k + 1) * P], c["ident"][0:Q, 0:Q])
                    last.then_inc(s["pe"], 1)
                pe.wait_ge(s["filled"], 3)
                t.matmul(ps_h[:, :], zero_b[:, :], zero_b[:, 0:NT], start=True, stop=False)

                def count(b, u):
                    pe.wait_ge(s["hot"], b + 1)
                    pe.wait_ge(s["hot_hi"], b + 1)
                    for g in range(G):
                        last = t.matmul(ps_h[:, :], hot_lo[u][:, g, :], hot_hi[u][:, g, :], start=False, stop=False)
                    last.then_inc(s["counted"], 1)

                with pe.Fori(0, HALF) as i:
                    count(i * 2, 0)
                    count(i * 2 + 1, 1)
                t.matmul(ps_h[:, :], zero_b[:, :], zero_b[:, 0:NT], start=False, stop=True).then_inc(s["counted"], 1)
                pe.wait_ge(s["dv"], 18)
                t.matmul(ps_s[:, 64:64 + NT], c["before"][:, :], has[:, :], start=True, stop=True)
                t.matmul(ps_s[:, 128:128 + NT], c["ones"][:, :], has[:, :], start=True, stop=True).then_inc(s["pe"], 1)

            @block.scalar
            def _(act):
                def hots(b, u, i):
                    act.wait_ge(s["off_hi"], b + 1)
                    off = off_hi[u][:, :, :]
                    nc.scalar.activation(off, off, ACT.Square).then_inc(s["squared"], 1)
                    if i is not None:
                        act.wait_ge(s["counted"], b - 1)
                    act.wait_ge(s["squared"], b + 1)
                    nc.scalar.activation(hot_hi[u][:, :, :], off, ACT.Relu, bias=c["ones"][:, 0:1], scale=-1.0).then_inc(s["hot_hi"], 1)

                hots(0, 0, None)
                hots(1, 1, None)
                with act.Fori(1, HALF) as i:
                    hots(i * 2, 0, i)
                    hots(i * 2 + 1, 1, i)

            @block.gpsimd
            def _(pool):
                g = nc.gpsimd
                g.memset(xr[:, :, :], 0.0).then_inc(s["filled"], 1)
                g.memset(nt_i[:, :], 0).then_inc(s["filled"], 1)
                g.memset(zero_b[:, :], 0.0).then_inc(s["filled"], 1)
                g.iota(n_i[:, :], [[P, NT]], base=0, channel_multiplier=1).then_inc(s["filled"], 1)
                pool.wait_ge(s["dv"], 17)

                def offsets(b, u, i):
                    if i is not None:
                        pool.wait_ge(s["hot_hi"], b - 1)
                    g.tensor_tensor(off_hi[u][:, :, :], row_b[:, 0:NT].rearrange("p (o e) -> p o e", o=1).to_broadcast([P, G, NT]),
                                    hi_t[:, bass.ds(b * G, G)].rearrange("p (g o) -> p g o", o=1).to_broadcast([P, G, NT]),
                                    ALU.subtract).then_inc(s["off_hi"], 1)

                offsets(0, 0, None)
                offsets(1, 1, None)
                with pool.Fori(1, HALF) as i:
                    offsets(i * 2, 0, i)
                    offsets(i * 2 + 1, 1, i)
                pool.wait_ge(s["dv"], 31)
                for i in range(NT):
                    g.indirect_dma_start(out=scratch["rows"][:, :], out_offset=bass.IndirectOffsetOnAxis(ap=compact[:, i:i + 1], axis=0),
                                         in_=xr[:, i, :], in_offset=None).then_inc(s["scattered"], 16)
                pool.wait_ge(s["scattered"], 16 * NT)



def node_stage(nc, c, s, put_out, spent, l, tab, scratch, acc, weights, out):
    q_out, h_out = ([s[f"{x}_out{u}"] for u in range(2)] if l < L else None for x in "qh")
    first, last = l == 0, l == L
    PAIRS = NT // 2
    P2 = 2 * P
    HALF_R = R * 2 * HS
    NORM = 9 if first else 13
    VAR = 5 if first else 8
    TURN = 1 if last else 2
    LIN = TURN + 2
    with ExitStack() as st:
        sb = lambda n, sh, d=F32: st.enter_context(nc.sbuf_tensor(f"n{l}_{n}", sh, d))
        pb = lambda n, sh: st.enter_context(nc.psum_tensor(f"n{l}_{n}", sh, F32))
        final = [sb(f"final{u}", [P, 2, D]) for u in range(2)]
        type_row = sb("type_row", [P, NP], BF16)
        stats, mean_var = sb("stats", [P, 2, 6]), sb("mean_var", [P, 2, 2])
        var, rstd = sb("var", [P, 2]), sb("rstd", [P, 2])
        if first:
            type_b = sb("type_b", [P, NT], BF16)
        if first:
            xr = acc[:, :, :].rearrange("p a n -> p (a n)")[:, 0:NT * XW].rearrange("p (t d) -> p t d", d=XW)
        if last:
            xr = sb("xr", [P, NT, XW])
        if not first:
            h = sb("h", [P, NT, D])
            act_out = [sb(f"act_out{u}", [P, 2, D]) for u in range(2)]
            skip, al, gain, shift = sb("skip", [P, TN]), sb("al", [P, NT]), sb("gain", [P, D]), sb("shift", [P, D])
            by_type = sb("by_type", [P, NT, TN])
            agg, agg_k, wa = sb("agg", [P, P2]), sb("agg_k", [P, TN, P2]), sb("wa", [P, TN, D])
            ps_lin = pb("ps_lin", [P, 2, 256])
        ids = [sb(f"ids{u}", [P, 1], I32) for u in range(2)]
        ps_turn = pb("ps_turn", [P, 2, 256])
        if not last:
            wk, wv, wq = (sb(n, [P, TN, D]) for n in ("wk", "wv", "wq"))
            bd = [sb(f"bd{i}", [P, R, 2 * HS]) for i in range(2)]
            pri = sb("pri", [P, R])
            ht = [sb(f"ht{u}", [P, TN, P2]) for u in range(2)]
            kv_t = sb("kv_t", [P, 2, P2])
            q_sb = [sb(f"q_sb{u}", [P, 2, D]) for u in range(2)]
            kv = [sb(f"kv{u}", [P, R, 2, D]) for u in range(2)]
            ps_kv, ps_q, ps_rel = pb("ps_kv", [P, 2, P2]), pb("ps_q", [P, 2, 256]), pb("ps_rel", [P, 4, 2, HALF_R])
        else:
            wff, bff = sb("wff", [P, D]), sb("bff", [P, D])
            ht = [sb(f"ht{u}", [P, 2, P]) for u in range(2)]
            y = [sb(f"y{u}", [P, D]) for u in range(2)]
            ps_y = [pb(f"ps_y{u}", [P, 512]) for u in range(2)]

        def over(engine, step):
            start, stop = 1, PAIRS - 4
            for p in range(-LIN, start):
                step(p, p % 2, p // 2)
            with engine.Fori(0, (stop - start) // 2) as i:
                for n in range(2):
                    step(i * 2 + (start + n), (start + n) % 2, i + (start + n) // 2)
            for p in range(stop, PAIRS):
                step(p, p % 2, p // 2)

        def real(p):
            return not isinstance(p, int) or 0 <= p < PAIRS

        def early(p, n):
            return isinstance(p, int) and p < n

        def pair(a, p):
            return a[:, bass.ds(p * 2, 2), :]

        def cols(p):
            return bass.ds(p * P2, P2)

        def store_rows(engine, u):
            act = engine == "act"
            for q in ((0, 1) if act else (2, 3)):
                to = kv[u][:, :, :, q * 32:(q + 1) * 32].rearrange("p r a f -> p a r f")
                of = ps_rel[:, q, :, :].rearrange("p a (r f) -> p a r f", r=R)
                ins = nc.scalar.activation(to, of, ACT.Copy) if act else nc.vector.tensor_copy(to, of)
            ins.then_inc(s["rel_a" if act else "rel_v"], 1)

        with nc.Block() as block:
            @block.vector
            def _(dve):
                v = nc.vector
                n = [0]

                def did(ins):
                    ins.then_inc(s["dv"], 1)
                    n[0] += 1

                def then(ins):
                    did(ins)
                    dve.wait_ge(s["dv"], n[0])

                if not last:
                    v.memset(bd[0][:, :, :], 0.0).then_inc(s["built"], 1)
                    v.memset(bd[1][:, :, :], 0.0).then_inc(s["built"], 1)
                if first:
                    dve.wait_ge(s["rows"], 16)
                    did(v.tensor_copy(type_b[:, :], xr[:, :, D]))
                    did(v.tensor_copy(tab["id"][:, :], xr[:, :, D + 1]))
                    did(v.tensor_tensor(tab["type"][:, :, :], xr[:, :, D:D + 1].to_broadcast([P, NT, TN]),
                                        c["type_iota"][:, :].rearrange("p (o t) -> p o t", o=1).to_broadcast([P, NT, TN]),
                                        ALU.is_equal))
                else:
                    dve.wait_ge(s["gates"], 1)
                    then(v.tensor_tensor(by_type[:, :, :], tab["type"][:, :, :],
                                         skip[:, :].rearrange("p (o t) -> p o t", o=1).to_broadcast([P, NT, TN]), ALU.mult))
                    did(v.reduce_sum(al[:, :], by_type[:, :, :], axis=AX.X))
                if last:
                    dve.wait_ge(s["rows"], 32)
                    dve.wait_ge(s["w"], 96)
                    did(v.tensor_tensor(xr[:, :, 0:D], xr[:, :, 0:D],
                                        bff[:, :].rearrange("p (o d) -> p o d", o=1).to_broadcast([P, NT, D]), ALU.add))
                dve.wait_ge(s["dv"], n[0])

                def scale_relations():
                    dve.wait_ge(s["bd"], 16 * (3 * H))
                    then(v.tensor_scalar(pri[:, :], pri[:, :], float(HS) ** -0.5, None, ALU.mult))
                    v.tensor_tensor(bd[0][:, :, :], bd[0][:, :, :],
                                    pri[:, :].rearrange("p (r o) -> p r o", o=1).to_broadcast([P, R, 2 * HS]),
                                    ALU.mult).then_inc(s["built"], 1)

                def masks(to, of, p, signal):
                    for k in range(TN):
                        ins = v.scalar_tensor_tensor(out=to[:, k, :], in0=type_row[:, cols(p)], scalar=float(k), in1=of,
                                                     op0=ALU.is_equal, op1=ALU.mult)
                    ins.then_inc(s[signal], 1)

                def aggregate(p):
                    if not early(p, 1):
                        dve.wait_ge(s["agg_k"], p)
                    v.tensor_scalar(agg[:, :], acc[:, 1, cols(p)], 1e-16, None, ALU.add).then_inc(s["agg"], 1)
                    dve.wait_ge(s["agg"], p * 3 + 1)
                    v.reciprocal(agg[:, :], agg[:, :]).then_inc(s["agg"], 1)
                    dve.wait_ge(s["agg"], p * 3 + 2)
                    v.tensor_tensor(agg[:, :], agg[:, :], acc[:, 0, cols(p)], ALU.mult).then_inc(s["agg"], 1)
                    if early(p, 1):
                        dve.wait_ge(s["type_row"], 16)
                    else:
                        dve.wait_ge(s["lin"], p)
                    dve.wait_ge(s["agg"], p * 3 + 3)
                    masks(agg_k, agg[:, :], p, "agg_k")

                def normed(p, k):
                    def then(ins, wait=True):
                        k[0] += 1
                        ins.then_inc(s["norm"], 1)
                        if wait:
                            dve.wait_ge(s["norm"], p * NORM + k[0])
                    return then

                def variance(p, u):
                    then = normed(p, [0])
                    if not first:
                        hp = pair(h, p)
                        if early(p, 1):
                            dve.wait_ge(s["rows"], 32 if last else 16)
                        dve.wait_ge(s["silu"], p + 1)
                        s_ = act_out[u][:, :, :]
                        then(v.tensor_tensor(s_, s_, hp, ALU.subtract))
                        then(v.tensor_tensor(s_, s_, al[:, bass.ds(p * 2, 2)].rearrange("p (t o) -> p t o", o=1).to_broadcast([P, 2, D]), ALU.mult))
                        then(v.tensor_tensor(hp, hp, s_, ALU.add))
                    of = xr if first else h
                    dve.sem_inc(s["bn"], 1)
                    for j in range(2):
                        then(v.bn_stats(stats[:, j, :], of[:, bass.ds(p * 2 + j, 1), 0:D].rearrange("p o d -> p (o d)")), wait=j == 1)
                    dve.sem_inc(s["bn"], 1)
                    for j in range(2):
                        then(v.bn_aggr(mean_var[:, j, :], stats[:, j, :]), wait=j == 1)
                    then(v.tensor_scalar(var[:, :], mean_var[:, :, 1], EPS, None, ALU.add), wait=False)

                def normalise(p, u, stores):
                    then = normed(p, [VAR])
                    of = xr if first else h
                    if not early(p, 2):
                        dve.wait_ge(s["turn"], p - 1)
                        if not last:
                            dve.wait_ge(h_out[u], stores)
                    dve.wait_ge(s["root"], p + 1)
                    then(v.reciprocal(rstd[:, :], var[:, :]))
                    for j in range(2):
                        then(v.tensor_scalar(final[u][:, j, :], of[:, bass.ds(p * 2 + j, 1), 0:D].rearrange("p o d -> p (o d)"),
                                             mean_var[:, j, 0:1], rstd[:, j:j + 1], ALU.subtract, ALU.mult), wait=j == 1)
                    f = final[u][:, :, :]
                    if first:
                        then(v.tensor_scalar(f, f, 0.0, None, ALU.max), wait=False)
                    else:
                        for a, op in ((gain, ALU.mult), (shift, ALU.add)):
                            then(v.tensor_tensor(f, f, a[:, :].rearrange("p (o d) -> p o d", o=1).to_broadcast([P, 2, D]), op), wait=a is gain)

                def rows_out(p, j):
                    dve.wait_ge(s["rel"], p * 2 + j + 1)
                    if not early(p, 1):
                        dve.wait_ge(put_out[j], p * 16)
                    store_rows("dve", j)

                def parts(p, u):
                    if early(p, 1) and first:
                        dve.wait_ge(s["type_row"], 16)
                    if not early(p, 2):
                        dve.wait_ge(s["kv_ps"], p - 1)
                    dve.wait_ge(s["turn"], p + 1)
                    masks(ht[u], ps_turn[:, 0, :], p, "ht")

                def result(p, j):
                    dve.wait_ge(s["y_ps"], p * 2 + j + 1)
                    if not early(p, 1):
                        dve.wait_ge(put_out[j], p * 16)
                    v.tensor_tensor(y[j][:, :], ps_y[j][:, 0:D], xr[:, bass.ds(p * 2 + j, 1), 0:D].rearrange("p o d -> p (o d)"),
                                    ALU.add).then_inc(s["y"], 1)

                def step(p, u, w):
                    if isinstance(p, int) and p == -1 and not last:
                        scale_relations()
                    if real(p + TURN):
                        variance(p + TURN, (u + TURN) % 2)
                    if real(p) and not last:
                        rows_out(p, 0)
                    if real(p + LIN) and not first:
                        aggregate(p + LIN)
                    if real(p + TURN):
                        normalise(p + TURN, (u + TURN) % 2, (w + 1) * 16)
                    if real(p):
                        if last:
                            result(p, 0)
                            result(p, 1)
                        else:
                            rows_out(p, 1)
                    if real(p + TURN) and not last:
                        parts(p + TURN, (u + TURN) % 2)

                over(dve, step)

            @block.sync
            def _(sp):
                spent.clear(sp)

                def load(to, of, sm):
                    sp.dma_start(to, of).then_inc(sm, 16)

                tiles = lambda a: a.rearrange("(t p) d -> p t d", p=P)
                if first or last:
                    load(xr[:, :, :], tiles(scratch["rows"]), s["rows"])
                if first:
                    sp.wait_ge(s["dv"], 1)
                    with nc.allow_non_contiguous_dma(reason="one word for each node, once"):
                        load(scratch["type"].rearrange("(t p) -> p t", p=P), type_b[:, :], s["type_out"])
                    sp.wait_ge(s["type_out"], 16)
                load(type_row[:, :], scratch["type"].rearrange("(o n) -> o n", o=1).to_broadcast([P, NP]), s["type_row"])
                if not first:
                    load(skip[:, :], weights["skip"][l - 1:l, :].to_broadcast([P, TN]), s["w"])
                    load(wa[:, :, :], weights["Wa"][l - 1].rearrange("t i o -> i t o"), s["w"])
                    load(gain[:, :], weights["ln_g"][l - 1:l, :].to_broadcast([P, D]), s["w"])
                    load(shift[:, :], weights["ln_b"][l - 1:l, :].to_broadcast([P, D]), s["w"])
                    load(h[:, :, :], tiles(scratch["h"]), s["rows"])
                if last:
                    load(wff[:, :], weights["Wff"], s["w"])
                    load(bff[:, :], weights["bff"].rearrange("(o d) -> o d", o=1).to_broadcast([P, D]), s["w"])
                    return
                for to, name in ((wk, "Wk"), (wv, "Wv"), (wq, "Wq")):
                    load(to[:, :, :], weights[name][l].rearrange("t i o -> i t o"), s["w_kvq"])
                sp.wait_ge(s["built"], 2)
                with nc.allow_non_contiguous_dma(reason="small weights, once"):
                    for i, name in enumerate(("Watt", "Wmsg")):
                        for hd in range(H):
                            at = hd % 2 * HS
                            load(bd[i][hd * HS:(hd + 1) * HS, :, at:at + HS], weights[name][l, hd].rearrange("r i o -> i r o"), s["bd"])
                    for hd in range(H):
                        load(pri[hd * HS:(hd + 1) * HS, :], weights["pri"][l, hd:hd + 1, :].to_broadcast([HS, R]), s["bd"])
                if not first:
                    sp.wait_ge(s["rows"], 16)
                h_d, q_d = tiles(scratch["h"]), tiles(scratch["q"])

                def step(p, u, w):
                    if real(p + TURN):
                        sp.wait_ge(s["norm"], (p + TURN + 1) * NORM)
                        load(h_d[:, bass.ds(p * 2 + 2 * TURN, 2), :], final[u][:, :, :], h_out[u])
                    if real(p + 1):
                        sp.wait_ge(s["q_sb"], p + 2)
                        load(q_d[:, bass.ds(p * 2 + 2, 2), :], q_sb[1 - u][:, :, :], q_out[1 - u])

                over(sp, step)
                for u in range(2):
                    for out_u in (h_out[u], q_out[u]):
                        sp.wait_ge(out_u, 16 * ((PAIRS + 1 - u) // 2))

            @block.scalar
            def _(act):
                a = nc.scalar
                if not first:
                    act.wait_ge(s["w"], 96 if last else 64)
                    a.activation(skip[:, :], skip[:, :], ACT.Sigmoid).then_inc(s["gates"], 1)

                def root(p):
                    act.wait_ge(s["norm"], p * NORM + VAR)
                    a.activation(var[:, :], var[:, :], ACT.Sqrt).then_inc(s["root"], 1)

                def silu(p, u):
                    act.wait_ge(s["lin"], p + 1)
                    a.activation(act_out[u][:, :, :], ps_lin[:, 0, :].rearrange("p (t d) -> p t d", t=2), ACT.Silu).then_inc(s["silu"], 1)

                def rows_out(p, j):
                    act.wait_ge(s["rel"], p * 2 + j + 1)
                    if not early(p, 1):
                        act.wait_ge(put_out[j], p * 16)
                    store_rows("act", j)

                def q_copy(p, u, turns):
                    act.wait_ge(s["q_ps"], p + 1)
                    if not early(p, 2):
                        act.wait_ge(q_out[u], turns)
                    a.activation(q_sb[u][:, :, :], ps_q[:, 0, :].rearrange("p (t d) -> p t d", t=2), ACT.Copy).then_inc(s["q_sb"], 1)

                def kv_copy(p):
                    act.wait_ge(s["kv_ps"], p + 1)
                    if not early(p, 1):
                        act.wait_ge(s["rel"], p * 2)
                    a.activation(kv_t[:, :, :], ps_kv[:, :, :], ACT.Copy).then_inc(s["kv_t"], 1)

                def turned(p, u):
                    act.wait_ge(s["turn"], p + 1)
                    if not early(p, 2):
                        act.wait_ge(s["y_ps"], p * 2 - 2)
                    a.activation(ht[u][:, :, :], ps_turn[:, 0, :].rearrange("p (t n) -> p t n", t=2), ACT.Copy).then_inc(s["ht"], 1)

                def step(p, u, w):
                    if last:
                        if real(p + TURN):
                            root(p + TURN)
                        if real(p + LIN):
                            silu(p + LIN, (u + LIN) % 2)
                        if real(p + TURN):
                            turned(p + TURN, (u + TURN) % 2)
                        return
                    if real(p):
                        rows_out(p, 0)
                    if real(p + TURN):
                        root(p + TURN)
                    if real(p + 1):
                        q_copy(p + 1, 1 - u, (w + u) * 16)
                    if real(p):
                        rows_out(p, 1)
                    if real(p + 1):
                        kv_copy(p + 1)
                    if real(p + LIN) and not first:
                        silu(p + LIN, (u + LIN) % 2)

                over(act, step)

            @block.tensor
            def _(pe):
                t_ = nc.tensor
                if not first:
                    pe.wait_ge(s["w"], 96 if last else 64)
                if not last:
                    pe.wait_ge(s["w_kvq"], 48)

                def lin(p):
                    pe.wait_ge(s["agg_k"], p + 1)
                    if not early(p, 1):
                        pe.wait_ge(s["silu"], p)
                    for j in range(2):
                        for k in range(TN):
                            ins = t_.matmul(ps_lin[:, 0, j * P:(j + 1) * P], agg_k[:, k, j * P:(j + 1) * P], wa[:, k, :],
                                            start=k == 0, stop=k == TN - 1)
                    ins.then_inc(s["lin"], 1)

                def turn(p, u):
                    pe.wait_ge(s["norm"], (p + 1) * NORM)
                    if not early(p, 1):
                        pe.wait_ge(s["ht"], p)
                    for j in range(2):
                        ins = t_.transpose(ps_turn[:, 0, j * P:(j + 1) * P], final[u][:, j, :],
                                           c["ident"][:, :])
                    ins.then_inc(s["turn"], 1)

                def typed_q(p, u):
                    pe.wait_ge(s["ht"], p + 1)
                    if not early(p, 1):
                        pe.wait_ge(s["q_sb"], p)
                    for j in range(2):
                        for k in range(TN):
                            ins = t_.matmul(ps_q[:, 0, j * P:(j + 1) * P], ht[u][:, k, j * P:(j + 1) * P], wq[:, k, :],
                                            start=k == 0, stop=k == TN - 1)
                    ins.then_inc(s["q_ps"], 1)

                def typed_kv(p, u):
                    if not early(p, 1):
                        pe.wait_ge(s["kv_t"], p)
                    for a, w in enumerate((wk, wv)):
                        for k in range(TN):
                            ins = t_.matmul(ps_kv[:, a, :], w[:, k, :], ht[u][:, k, :], start=k == 0, stop=k == TN - 1)
                    ins.then_inc(s["kv_ps"], 1)

                def related(p, j):
                    pe.wait_ge(s["kv_t"], p + 1)
                    if early(p, 1) and j == 0:
                        pe.wait_ge(s["built"], 3)
                    if not (early(p, 1) and j == 0):
                        pe.wait_ge(s["rel_a"], p * 2 + j)
                        pe.wait_ge(s["rel_v"], p * 2 + j)
                    for a in range(2):
                        for q in range(4):
                            rows = slice(q * 32, (q + 1) * 32)
                            ins = t_.matmul(ps_rel[:, q, a, :], kv_t[rows, a, j * P:(j + 1) * P],
                                            bd[a][rows, :, :].rearrange("p r f -> p (r f)"), start=True, stop=True)
                    ins.then_inc(s["rel"], 1)

                def project(p, u):
                    pe.wait_ge(s["ht"], p + 1)
                    for j in range(2):
                        if not early(p, 1):
                            pe.wait_ge(s["y"], p * 2 + j - 1)
                        t_.matmul(ps_y[j][:, 0:D], ht[u][:, j, :], wff[:, :], start=True, stop=True).then_inc(s["y_ps"], 1)

                def step(p, u, w):
                    if last:
                        if real(p):
                            project(p, u)
                        if real(p + LIN):
                            lin(p + LIN)
                        if real(p + TURN):
                            turn(p + TURN, (u + TURN) % 2)
                        return
                    if real(p):
                        related(p, 0)
                    if real(p + 1):
                        typed_q(p + 1, 1 - u)
                    if real(p):
                        related(p, 1)
                    if real(p + TURN) and not first:
                        turn(p + TURN, (u + TURN) % 2)
                    if real(p + 1):
                        typed_kv(p + 1, 1 - u)
                    if real(p + LIN) and not first:
                        lin(p + LIN)
                    if real(p + TURN) and first:
                        turn(p + TURN, (u + TURN) % 2)

                over(pe, step)

            @block.gpsimd
            def _(pool):
                g = nc.gpsimd
                if first:
                    pool.wait_ge(s["dv"], 2)

                def put(i, u, peeled=False):
                    t = i * 2 + u
                    if not peeled:
                        pool.wait_ge(put_out[u], i * 16)
                    g.tensor_copy(ids[u][:, :], tab["id"][:, bass.ds(t, 1)]).then_inc(s["id"], 1)
                    pool.wait_ge(s["id"], t + 1)
                    pool.wait_ge(s["y" if last else "rel_a"], t + 1)
                    if not last:
                        pool.wait_ge(s["rel_v"], t + 1)
                    pool.sem_inc(s["go"], 1)
                    if last:
                        g.indirect_dma_start(out=out[:, :], out_offset=bass.IndirectOffsetOnAxis(ap=ids[u][:, :], axis=0),
                                             in_=y[u][:, :], in_offset=None, bounds_check=N - 1, oob_is_err=False).then_inc(put_out[u], 16)
                    else:
                        g.indirect_dma_start(out=scratch["kv"].rearrange("(n r) d -> n (r d)", r=R),
                                             out_offset=bass.IndirectOffsetOnAxis(ap=ids[u][:, :], axis=0),
                                             in_=kv[u][:, :, :, :].rearrange("p r a d -> p (r a d)"), in_offset=None).then_inc(put_out[u], 16)

                put(0, 0, True)
                put(0, 1, True)
                with pool.Fori(1, NT // 2) as i:
                    for u in range(2):
                        put(i, u)
                for u in range(2):
                    pool.wait_ge(put_out[u], 8 * NT)


def edge_stage(nc, c, s, rows_in, spent, l, tab, scratch, acc):
    q_in = [s[f"q_in{u}"] for u in range(2)]
    TP = G // 2
    EARLY = 8
    FOUR = 4
    NF = -(-G // FOUR)
    fours = [range(FOUR * k, min(G, FOUR * (k + 1))) for k in range(NF)]
    with ExitStack() as st:
        sb = lambda n, sh, d=F32: st.enter_context(nc.sbuf_tensor(f"g{l}_{n}", sh, d))
        pb = lambda n, sh: st.enter_context(nc.psum_tensor(f"g{l}_{n}", sh, F32))
        ids = [sb(f"ids{j}", [P, G], I32) for j in range(U)]
        rows = [sb(f"rows{j}", [P, G, 2 * D]) for j in range(U)]
        qw = [sb(f"qw{u}", [P, G, D]) for u in range(2)]
        hot = [sb(f"hot{j}", [P, G, P]) for j in range(U)]
        hot_t = sb("hot_t", [P, G, P])
        score = sb("score", [P, G, H])
        fwd, top, m, shifted, exp_t = (sb(n, [GH, P]) for n in ("fwd", "top", "m", "shifted", "exp_t"))
        ends = sb("ends", [GH, 2, G])
        carry = [sb(f"carry{u}", [H, G + 1]) for u in range(2)]
        into, top1, delta, grown = (sb(n, [H, G]) for n in ("into", "top1", "delta", "grown"))
        into_x = sb("into_x", [H, G, H])
        seam = sb("seam", [GH, P + 1], BF16)
        scale = [sb(f"scale{u}", [P, G]) for u in range(2)]
        firsts = [sb(f"firsts{u}", [P, G, 2]) for u in range(2)]
        ps_q = [pb(f"ps_q{u}", [P, FOUR, D]) for u in range(2)]
        ps_hot = [pb(f"ps_hot{u}", [P, FOUR, P]) for u in range(2)]
        ps_sum = [pb(f"ps_sum{u}", [P, 2, 2, P]) for u in range(2)]
        for_dve, for_act = pb("ps_dve", [P, 512]), pb("ps_act", [P, 512])
        score_t, ends_ps, into_ps = for_dve[0:GH, 0:P], for_dve[0:H, 128:128 + 2 * G], for_dve[0:GH, 160:161]
        exp_ps, scale_ps = for_act[:, 0:GH], for_act[:, 128:128 + G]

        def over(engine, body, after, count=B):
            for j in range(U):
                body(0, j, j)
            with engine.Fori(1, count // U) as i:
                for j in range(U):
                    body(i, j, i * U + j)
            if after:
                after()

        def in_flight(i, j, b):
            whole = isinstance(b, int)
            return tuple(None if whole and not 0 <= b - n < B else (b - n, (j - n) % U) for n in range(3))

        def early(b, n):
            return isinstance(b, int) and b < n

        def windows(engine, regs, b, g):
            if g % 4 == 0:
                engine.reg_load(regs, tab["w0"][0:1, bass.ds(b * NB + g, 4)])
            return engine.snap(regs[g % 4], min_val=0, max_val=N)

        with nc.Block() as block:
            @block.sync
            def _(sp):
                spent.clear(sp)
                regs = [sp.alloc_register(f"sp_window{l}_{k}") for k in range(4)]

                def batch(i, j, b):
                    u = j % 2
                    if not early(b, 2):
                        sp.wait_ge(s["spread"], (b - 1) * NF)
                    for g in range(G):
                        w = windows(sp, regs, b, g)
                        sp.dma_start(qw[u][:, g, :], scratch["q"][bass.ds(w, P), :]).then_inc(q_in[u], 16)

                over(sp, batch, None)

            @block.gpsimd
            def _(pool):
                g_ = nc.gpsimd

                def batch(i, j, b):
                    if not early(b, U):
                        pool.wait_ge(s["sums"], (b - U + 1) * TP)
                    g_.tensor_copy(ids[j][:, :], tab["key"][:, bass.ds(b * G, G)]).then_inc(s["ids"], 1)
                    pool.wait_ge(s["ids"], b + 1)
                    pool.sem_inc(s["go"], 1)
                    for g in range(G):
                        g_.indirect_dma_start(out=rows[j][:, g, :], out_offset=None, in_=scratch["kv"][:, :],
                                              in_offset=bass.IndirectOffsetOnAxis(ap=ids[j][:, g:g + 1], axis=0)).then_inc(rows_in[2 * j + (g >= EARLY)], 16)
                    if isinstance(b, int) and b == 0:
                        g_.memset(acc[:, :, :], 0.0).then_inc(s["zeroed"], 1)
                        for u in range(2):
                            g_.memset(carry[u][:, :], -BIG).then_inc(s["zeroed"], 1)

                over(pool, batch, None)

            @block.vector
            def _(dve):
                v = nc.vector
                regs = [dve.alloc_register(f"dve_window{l}_{k}") for k in range(4)]

                def one_hot(b, j):
                    if not early(b, U):
                        dve.wait_ge(s["sums"], (b - U + 1) * TP)
                    v.tensor_tensor(hot[j][:, :, :], c["row"][:, :].rearrange("p (o e) -> p o e", o=1).to_broadcast([P, G, P]),
                                    tab["rank"][:, bass.ds(b * G, G)].rearrange("p (g o) -> p g o", o=1).to_broadcast([P, G, P]),
                                    ALU.is_equal).then_inc(s["hot"], 1)

                def columns(b, j, some):
                    dve.wait_ge(s["copied"], b * G + some[-1] + 1)
                    for g in some:
                        w = windows(dve, regs, b, g)
                        if not (early(b, 1) and g == 0):
                            dve.wait_ge(s["column"], b * G + g)
                        at = acc[:, :, bass.ds(w, 1)]
                        v.scalar_tensor_tensor(out=at, in0=at, scalar=scale[j % 2][:, g:g + 1], in1=firsts[j % 2][:, g, :].rearrange("p (a o) -> p a o", o=1),
                                               op0=ALU.mult, op1=ALU.add).then_inc(s["column"], 1)

                def products(i, j, b, some):
                    for k in some:
                        four = fours[k]
                        if k == 0:
                            dve.wait_ge(rows_in[2 * j], (i + 1) * 16 * EARLY)
                        if k * FOUR == EARLY:
                            dve.wait_ge(rows_in[2 * j + 1], (i + 1) * 16 * (G - EARLY))
                        part = rows[j][:, four[0]:four[-1] + 1, 0:D]
                        dve.wait_ge(s["spread"], b * NF + k + 1)
                        v.tensor_tensor(part, part, ps_q[k % 2][:, 0:len(four), :], ALU.mult).then_inc(s["prod"], 1)

                def scores(j, b):
                    dve.wait_ge(s["prod"], b * NF + NF)
                    v.reduce_sum(score[:, :, :], rows[j][:, :, 0:D].rearrange("p g (h d) -> p g h d", h=H),
                                 axis=AX.X).then_inc(s["score"], 1)

                def own_maxima(b):
                    dve.wait_ge(s["score_t"], b + 1)
                    dve.wait_ge(s["seam"], b + 1)
                    v.tensor_tensor_scan(fwd[:, :], seam[:, 0:P], score_t, -BIG, ALU.add, ALU.max).then_inc(s["chain"], 1)
                    dve.wait_ge(s["chain"], b * CHAIN + 1)
                    v.tensor_tensor_scan(top[:, ::-1], seam[:, 1:P + 1][:, ::-1], fwd[:, ::-1], -BIG, ALU.add, ALU.max).then_inc(s["chain"], 1)
                    dve.wait_ge(s["chain"], b * CHAIN + 2)
                    v.tensor_tensor(ends[:, :, :], c["tile_mask"][:, :].rearrange("p (o g) -> p o g", o=1).to_broadcast([GH, 2, G]),
                                    top[:, 0:P:P - 1].rearrange("p (a o) -> p a o", o=1).to_broadcast([GH, 2, G]),
                                    ALU.mult).then_inc(s["ends"], 1)

                def carried(b, j):
                    if early(b, 1):
                        dve.wait_ge(s["zeroed"], 3)
                    dve.wait_ge(s["ends_ps"], b + 1)
                    ca, cb = carry[j % 2], carry[1 - j % 2]
                    v.tensor_copy(ca[:, 0:1], cb[:, G:G + 1]).then_inc(s["chain"], 1)
                    v.tensor_tensor_scan(ca[:, 1:G + 1], tab["pass"][:, bass.ds(b * G, G)], ends_ps[:, G:2 * G],
                                         cb[:, G:G + 1], ALU.add, ALU.max).then_inc(s["chain"], 1)
                    dve.wait_ge(s["chain"], b * CHAIN + 4)
                    v.tensor_tensor(into[:, :], ca[:, 0:G], tab["new"][:, bass.ds(b * G, G)], ALU.add).then_inc(s["chain"], 1)
                    dve.wait_ge(s["chain"], b * CHAIN + 5)
                    v.tensor_tensor(top1[:, :], into[:, :], ends_ps[:, 0:G], ALU.max).then_inc(s["chain"], 1)
                    v.tensor_tensor(into_x[:, :, :], into[:, :].rearrange("p (g o) -> p g o", o=1).to_broadcast([H, G, H]),
                                    c["ident"][0:H, 0:H].rearrange("p (o h) -> p o h", o=1).to_broadcast([H, G, H]),
                                    ALU.mult).then_inc(s["carry"], 1)
                    dve.wait_ge(s["chain"], b * CHAIN + 6)
                    v.tensor_tensor(delta[:, :], into[:, :], top1[:, :], ALU.subtract).then_inc(s["scale"], 1)

                def shift(b):
                    dve.wait_ge(s["carry_ps"], b + 1)
                    v.tensor_tensor_scan(m[:, :], seam[:, 0:P], top[:, :], into_ps, ALU.add, ALU.max).then_inc(s["chain"], 1)
                    dve.wait_ge(s["chain"], b * CHAIN + 7)
                    v.tensor_tensor(shifted[:, :], score_t, m[:, :], ALU.subtract).then_inc(s["shifted"], 1)

                def messages(b, j):
                    dve.wait_ge(s["exp_sb"], b + 1)
                    v.tensor_tensor(rows[j][:, :, D:2 * D], rows[j][:, :, D:2 * D], rows[j][:, :, 0:D], ALU.mult).then_inc(s["message"], 1)

                def step(i, j, b):
                    new, mid, old = in_flight(i, j, b)
                    if mid:
                        own_maxima(mid[0])
                    if new:
                        products(i, j, b, [0])
                    if mid:
                        carried(*mid)
                    if new and in_flight(i, j + 1, b + 1)[0]:
                        one_hot(b + 1, (j + 1) % U)
                    if mid:
                        shift(mid[0])
                    if new:
                        products(i, j, b, [1])
                    if old:
                        columns(*old, range(0, 4))
                    if new:
                        products(i, j, b, [2])
                    if old:
                        columns(*old, range(4, 8))
                    if new:
                        products(i, j, b, [3])
                        scores(j, b)
                    if mid:
                        messages(*mid)
                    if old:
                        columns(*old, range(8, G))

                one_hot(0, 0)

                def end():
                    for n in range(U + 2):
                        step(B // U - 1, n, B - U + n)

                over(dve, step, end, B - U)
                dve.wait_ge(s["column"], T)

            @block.scalar
            def _(act):
                a = nc.scalar
                regs = [act.alloc_register(f"act_window{l}_{k}") for k in range(4)]

                def copies(b, j, some):
                    for g in some:
                        w = windows(act, regs, b, g)
                        ps = ps_sum[(j * TP + g // 2) % 2]
                        if g % 2 == 0:
                            act.wait_ge(s["sums"], b * TP + g // 2 + 1)
                            a.activation(firsts[j % 2][:, g:g + 2, :].rearrange("p g (a o) -> p g a o", o=1),
                                         ps[:, :, :, 0:1], ACT.Copy)
                        if early(b, 1) and g == 0:
                            act.wait_ge(s["zeroed"], 3)
                        else:
                            act.wait_ge(s["copied"], b * G + g)
                        a.activation(acc[:, :, bass.ds(w + 1, P - 1)], ps[:, g % 2, :, 1:P],
                                     ACT.Copy).then_inc(s["copied"], 1)

                def turned(b, some):
                    for k in some:
                        four = fours[k]
                        act.wait_ge(s["turned_ps"], b * NF + k + 1)
                        a.activation(hot_t[:, four[0]:four[-1] + 1, :], ps_hot[k % 2][:, 0:len(four), :], ACT.Copy).then_inc(s["turned"], 1)

                def flags(b):
                    if not early(b, 1):
                        act.wait_ge(s["chain"], b * CHAIN)
                    a.activation(seam[:, :], tab["seam"][:, bass.ds(b, 1), :].rearrange("p o e -> p (o e)"),
                                 ACT.Copy).then_inc(s["seam"], 1)

                def step(i, j, b):
                    new, mid, old = in_flight(i, j, b)
                    if new:
                        turned(b, range(0, 3))
                    if old:
                        copies(*old, range(0, 4))
                    if mid:
                        act.wait_ge(s["scale"], mid[0] + 1)
                        a.activation(grown[:, :], delta[:, :], ACT.Exp).then_inc(s["scale_sb"], 1)
                    if new:
                        turned(b, [3])
                    if old:
                        copies(*old, range(4, 8))
                    if mid:
                        act.wait_ge(s["scale_ps"], mid[0] + 1)
                        a.activation(scale[mid[1] % 2][:, :], scale_ps, ACT.Copy).then_inc(s["scale_sb"], 1)
                        act.wait_ge(s["shifted"], mid[0] + 1)
                        a.activation(exp_t[:, :], shifted[:, :], ACT.Exp).then_inc(s["exp_t"], 1)
                    if old:
                        copies(*old, range(8, 10))
                    if mid:
                        act.wait_ge(s["exp_ps"], mid[0] + 1)
                        a.activation(rows[mid[1]][:, :, 0:D].rearrange("p g (h d) -> p g h d", h=H),
                                     exp_ps.rearrange("p (g h o) -> p g h o", h=H, o=1).to_broadcast([P, G, H, HS]), ACT.Copy).then_inc(s["exp_sb"], 1)
                    if old:
                        copies(*old, range(10, G))
                    if new:
                        flags(b)

                def end():
                    for n in range(2):
                        step(B // U, n, B + n)

                over(act, step, end)

            @block.tensor
            def _(pe):
                t = nc.tensor

                def sums(b, j, some):
                    for g in some:
                        if g == 0:
                            pe.wait_ge(s["message"], b + 1)
                        if g % 2 == 0 and not (early(b, 1) and g < 4):
                            pe.wait_ge(s["copied"], b * G + g - 2)
                        ps = ps_sum[(j * TP + g // 2) % 2]
                        t.matmul(ps[:, g % 2, 0, :], rows[j][:, g, D:2 * D], hot[j][:, g, :], start=True, stop=True)
                        ins = t.matmul(ps[:, g % 2, 1, :], rows[j][:, g, 0:D], hot[j][:, g, :], start=True, stop=True)
                        if g % 2:
                            ins.then_inc(s["sums"], 1)

                def turn(b, j, some):
                    for k in some:
                        if k == 0:
                            pe.wait_ge(s["hot"], b + 1)
                        if not (early(b, 1) and k < 2):
                            pe.wait_ge(s["turned"], b * NF + k - 1)
                        for n, g in enumerate(fours[k]):
                            ins = t.transpose(ps_hot[k % 2][:, n, :], hot[j][:, g, :], c["ident"][:, :])
                        ins.then_inc(s["turned_ps"], 1)

                def spread(i, j, b, some):
                    for k in some:
                        if k == 0:
                            pe.wait_ge(q_in[j % 2], (i * 2 + j // 2 + 1) * 16 * G)
                        pe.wait_ge(s["turned"], b * NF + k + 1)
                        if not (early(b, 1) and k < 2):
                            pe.wait_ge(s["prod"], b * NF + k - 1)
                        for n, g in enumerate(fours[k]):
                            ins = t.matmul(ps_q[k % 2][:, n, :], hot_t[:, g, :], qw[j % 2][:, g, :], start=True, stop=True)
                        ins.then_inc(s["spread"], 1)

                def step(i, j, b):
                    new, mid, old = in_flight(i, j, b)
                    if new:
                        turn(b, j, [0, 1])
                    if mid:
                        pe.wait_ge(s["score"], mid[0] + 1)
                        t.transpose(score_t, score[:, :, :].rearrange("p g h -> p (g h)"), c["ident"][:, :]).then_inc(s["score_t"], 1)
                    if new:
                        spread(i, j, b, [0])
                        turn(b, j, [2])
                    if old:
                        sums(*old, range(0, 4))
                    if mid:
                        pe.wait_ge(s["ends"], mid[0] + 1)
                        t.matmul(ends_ps, c["head_of_row"][:, :], ends[:, :, :].rearrange("p a g -> p (a g)"), start=True, stop=True).then_inc(s["ends_ps"], 1)
                    if new:
                        turn(b, j, [3])
                        spread(i, j, b, [1])
                    if old:
                        sums(*old, range(4, 8))
                    if mid:
                        pe.wait_ge(s["carry"], mid[0] + 1)
                        t.matmul(into_ps, into_x[:, :, :].rearrange("p g h -> p (g h)"), c["ones"][0:H, 0:1], start=True, stop=True).then_inc(s["carry_ps"], 1)
                        pe.wait_ge(s["scale_sb"], mid[0] * 2 + 1)
                        t.matmul(scale_ps, c["head_of_feature"][:, :], grown[:, :], start=True, stop=True).then_inc(s["scale_ps"], 1)
                    if new:
                        spread(i, j, b, [2])
                    if old:
                        sums(*old, range(8, 10))
                    if new:
                        spread(i, j, b, [3])
                    if mid:
                        pe.wait_ge(s["exp_t"], mid[0] + 1)
                        t.transpose(exp_ps, exp_t[:, :], c["ident"][0:GH, 0:GH]).then_inc(s["exp_ps"], 1)
                    if old:
                        sums(*old, range(10, G))

                def end():
                    for n in range(2):
                        step(B // U, n, B + n)

                over(pe, step, end)


CHAIN = 7


def gnn(nc: bass.Bass, x, src, dst, edge_type_8, node_type_8, Wk, Wq, Wv, Wa, pri, Watt, Wmsg, skip, ln_g, ln_b,
        Wff, bff, out):
    weights = dict(Wk=Wk, Wq=Wq, Wv=Wv, Wa=Wa, pri=pri, Watt=Watt, Wmsg=Wmsg, skip=skip, ln_g=ln_g, ln_b=ln_b,
                   Wff=Wff, bff=bff)
    dram = lambda n, sh, d=F32: nc.dram_tensor(n, sh, d, kind="Internal").ap()
    edge_dst, edge_key = dram("edge_dst", [EP + 1], I32), dram("edge_key", [EP], I32)
    scratch = dict(w0=dram("window_starts", [B * NB], I32), rank=dram("edge_rank", [EP]), new=dram("tile_new", [T], BF16),
                   pas=dram("tile_pass", [T], BF16), type=dram("node_type_row", [NP], BF16), rows=dram("node_rows", [NP, XW]), h=dram("node_h", [NP, D]),
                   q=dram("node_q", [NP, D]), kv=dram("node_kv", [NP * R, 2 * D]))
    with ExitStack() as st:
        sb = lambda n, s, d=F32: st.enter_context(nc.sbuf_tensor(n, s, d))
        sem = lambda n: st.enter_context(nc.semaphore(n))
        c = constants(nc, sb, sem)
        tab = dict(key=sb("edge_key_sb", [P, T], I32), rank=sb("edge_rank_sb", [P, T]),
                   seam=sb("seam_flags", [GH, B, P + 1], BF16),
                   w0=sb("window_starts_sb", [1, B * NB], I32), new=sb("tile_new_sb", [H, T], BF16),
                   id=sb("node_id", [P, NT], I32), type=sb("node_type", [P, NT, TN]))
        tab["pass"] = sb("tile_pass_sb", [H, T], BF16)
        unsorted = sb("unsorted", [1, 1], I32)
        edge_lists(nc, sem, dst, src, edge_type_8, edge_dst, edge_key, unsorted)
        edge_sort(nc, c, sem, edge_dst, edge_key, unsorted, dram("dst_slots", [NP, 1]))
        edge_tables(nc, c, sem, x, node_type_8, edge_dst, edge_key, tab, scratch)
        acc = sb("acc", [P, 2, NP])
        own = lambda name, count: [sem(f"{name}{k}") for k in range(count)]
        nodes, edges = Signals(sem, "nodes"), Signals(sem, "edges")
        for l in range(L):
            node_stage(nc, c, nodes, own(f"nodes{l}_put", 2), edges, l, tab, scratch, acc, weights, out)
            edge_stage(nc, c, edges, own(f"edges{l}_rows_in", 2 * U), nodes, l, tab, scratch, acc)
        node_stage(nc, c, nodes, own(f"nodes{L}_put", 2), edges, L, tab, scratch, acc, weights, out)


_INS = ["x", "src", "dst", "edge_type_8", "node_type_8"] + ["L0_gnn_" + n for n in (
    "Wk", "Wq", "Wv", "Wa", "pri", "Watt", "Wmsg", "skip", "ln_g", "ln_b", "Wff", "bff")]


def kernel(**inputs):
    import numpy as _np
    import concourse.bacc as _bacc
    from concourse.bass_utils import run_bass_kernel_spmd as _run

    nc = _bacc.Bacc("TRN2", target_bir_lowering=False, num_devices=1)
    arrays, args = {}, []
    for name in _INS:
        a = _np.ascontiguousarray(inputs[name])
        arrays[f"in_{name}"] = a
        args.append(nc.dram_tensor(f"in_{name}", a.shape, mybir.dt.from_np(a.dtype), kind="ExternalInput").ap())
    out = nc.dram_tensor("out_nodes", (N, D), F32, kind="ExternalOutput").ap()
    gnn(nc, *args, out)
    r = _run(nc, [arrays], core_ids=[0])
    return r.results[0]["out_nodes"]
```
